# Optimizing a Trainium2 kernel written in Bass

```python
import numpy as np
import jax
import jax.numpy as jnp

def _softmax(x, axis=-1):
    return jax.nn.softmax(x, axis=axis)

def _gelu(x):
    return jax.nn.gelu(x, approximate=True)

def _silu(x):
    return jax.nn.silu(x)

def _sigmoid(x):
    return jax.nn.sigmoid(x)

def _layernorm(x, axis=-1, eps=1e-05):
    m = jnp.mean(x, axis=axis, keepdims=True)
    v = jnp.var(x, axis=axis, keepdims=True)
    return (x - m) / jnp.sqrt(v + eps)

def _scatter_add(tgt, idx, src, axis=0):
    return tgt.at[idx].add(src)

def _segment_sum(src, seg, n):
    return jax.ops.segment_sum(src, seg, n)
kernel_name = 'mk_prb_d2_jaxref_r8_eaea96'

def setup_inputs(seed: int=0):
    np.random.seed(seed)
    _w = jnp.asarray

    def _L0_attn_setup():
        import jax, jax.numpy as jnp
        import numpy as np
        N_HEADS = 32
        N_KV_HEADS = 8
        DIM = 512
        HEAD_DIM = DIM // N_HEADS
        N_REP = N_HEADS // N_KV_HEADS
        ROPE_THETA = 10000.0

        def _apply_rope(x):
            seq = x.shape[2]
            hd = x.shape[-1]
            inv_freq = 1.0 / ROPE_THETA ** (jnp.arange(0, hd, 2, dtype=jnp.float32) / hd)
            angles = jnp.arange(seq, dtype=jnp.float32)[:, None] * inv_freq[None, :]
            cos = jnp.cos(angles)[None, None]
            sin = jnp.sin(angles)[None, None]
            x1 = x[..., 0::2]
            x2 = x[..., 1::2]
            r1 = x1 * cos - x2 * sin
            r2 = x1 * sin + x2 * cos
            return jnp.stack([r1, r2], axis=-1).reshape(x.shape)
        key = jax.random.key(seed)
        k1, k2, k3 = jax.random.split(key, 3)
        bs, seq = (1, 256)
        x = jax.random.normal(k1, (bs, seq, DIM), dtype=jnp.float32)
        w_qkv = jax.random.normal(k2, (DIM, HEAD_DIM * (N_HEADS + 2 * N_KV_HEADS)), dtype=jnp.float32) * 0.02
        w_o = jax.random.normal(k3, (N_HEADS * HEAD_DIM, DIM), dtype=jnp.float32) * 0.02
        return {'x': x, 'w_qkv': w_qkv, 'w_o': w_o}
    _L0_attn_in = _L0_attn_setup()

    def _L0_ffn_setup():
        import jax, jax.numpy as jnp
        import numpy as np
        NUM_EXPERTS = 4
        HIDDEN = 512
        RANK = 8
        ALPHA = 8.0
        SCALE = ALPHA / RANK
        key = jax.random.key(seed)
        ks = jax.random.split(key, 6)
        B, T, H, E, R = (4, 512, HIDDEN, NUM_EXPERTS, RANK)
        x = jax.random.normal(ks[0], (B, T, H), dtype=jnp.float32)
        W_up = jax.random.normal(ks[1], (H, H), dtype=jnp.float32) / np.sqrt(H)
        gate_w = jax.random.normal(ks[2], (E, H), dtype=jnp.float32) / np.sqrt(H)
        expert_bias = jnp.zeros((E,), dtype=jnp.float32)
        lora_A = jax.random.normal(ks[3], (E, R, H), dtype=jnp.float32) / np.sqrt(H)
        lora_B = jax.random.normal(ks[4], (E, H, R), dtype=jnp.float32) * 0.01
        return {'x': x, 'W_up': W_up, 'gate_w': gate_w, 'expert_bias': expert_bias, 'lora_A': lora_A, 'lora_B': lora_B}
    _L0_ffn_in = _L0_ffn_setup()

    def _L1_attn_setup():
        import jax, jax.numpy as jnp
        import numpy as np
        H = 32
        HKV = 8
        D = 512
        HD = D // H
        S = 128
        MASK_OUT = 0.9
        MIN_REMAIN = 128
        THETA = 10000.0

        def rope_tables(seq_len, hd):
            inv_freq = 1.0 / THETA ** (jnp.arange(0, hd, 2, dtype=jnp.float32) / hd)
            t = jnp.arange(seq_len, dtype=jnp.float32)
            freqs = jnp.outer(t, inv_freq)
            emb = jnp.concatenate([freqs, freqs], axis=-1)
            return (jnp.cos(emb), jnp.sin(emb))

        def rotate_half(x):
            x1, x2 = jnp.split(x, 2, axis=-1)
            return jnp.concatenate([-x2, x1], axis=-1)

        def apply_rope(x, cos, sin):
            return x * cos + rotate_half(x) * sin
        key = jax.random.key(seed)
        k0, k1, k2, k3, k4 = jax.random.split(key, 5)
        hidden_states = jax.random.normal(k0, (1, S, D), jnp.float32)
        Wq = jax.random.normal(k1, (D, D), jnp.float32) * 0.02
        Wk = jax.random.normal(k2, (HKV * HD, D), jnp.float32) * 0.02
        Wv = jax.random.normal(k3, (HKV * HD, D), jnp.float32) * 0.02
        Wo = jax.random.normal(k4, (D, D), jnp.float32) * 0.02
        return {'hidden_states': hidden_states, 'Wq': Wq, 'Wk': Wk, 'Wv': Wv, 'Wo': Wo}
    _L1_attn_in = _L1_attn_setup()

    def _L1_ffn_setup():
        import jax, jax.numpy as jnp
        import numpy as np
        BLOCK = 64
        NF4_CODE = jnp.array([-1.0, -0.6961928009986877, -0.5250730514526367, -0.39491748809814453, -0.28444138169288635, -0.18477343022823334, -0.09105003625154495, 0.0, 0.07958029955625534, 0.16093020141124725, 0.24611230194568634, 0.33791524171829224, 0.44070982933044434, 0.5626170039176941, 0.7229568362236023, 1.0], dtype=jnp.float32)

        def dequant_nf4(q, absmax, shape):
            w = NF4_CODE[q.reshape(-1)]
            w = w.reshape(-1, BLOCK) * absmax[:, None]
            return w.reshape(shape)
        key = jax.random.key(seed)
        ks = jax.random.split(key, 7)
        HD, M = (512, 1792)
        nblk = HD * M // BLOCK
        x = jax.random.normal(ks[0], (2, 256, HD), dtype=jnp.float32)
        gate_q = jax.random.randint(ks[1], (M, HD), 0, 16, dtype=jnp.int32)
        up_q = jax.random.randint(ks[2], (M, HD), 0, 16, dtype=jnp.int32)
        down_q = jax.random.randint(ks[3], (HD, M), 0, 16, dtype=jnp.int32)
        gate_absmax = jax.random.uniform(ks[4], (nblk,), dtype=jnp.float32) * 0.05
        up_absmax = jax.random.uniform(ks[5], (nblk,), dtype=jnp.float32) * 0.05
        down_absmax = jax.random.uniform(ks[6], (nblk,), dtype=jnp.float32) * 0.05
        return {'x': x, 'gate_q': gate_q, 'gate_absmax': gate_absmax, 'up_q': up_q, 'up_absmax': up_absmax, 'down_q': down_q, 'down_absmax': down_absmax}
    _L1_ffn_in = _L1_ffn_setup()
    _d = {'L0_attn_x': _L0_attn_in['x'], 'L0_attn_w_qkv': _L0_attn_in['w_qkv'], 'L0_attn_w_o': _L0_attn_in['w_o'], 'L0_ffn_W_up': _L0_ffn_in['W_up'], 'L0_ffn_gate_w': _L0_ffn_in['gate_w'], 'L0_ffn_expert_bias': _L0_ffn_in['expert_bias'], 'L0_ffn_lora_A': _L0_ffn_in['lora_A'], 'L0_ffn_lora_B': _L0_ffn_in['lora_B'], 'L1_attn_Wq': _L1_attn_in['Wq'], 'L1_attn_Wk': _L1_attn_in['Wk'], 'L1_attn_Wv': _L1_attn_in['Wv'], 'L1_attn_Wo': _L1_attn_in['Wo'], 'L1_ffn_gate_q': _L1_ffn_in['gate_q'], 'L1_ffn_gate_absmax': _L1_ffn_in['gate_absmax'], 'L1_ffn_up_q': _L1_ffn_in['up_q'], 'L1_ffn_up_absmax': _L1_ffn_in['up_absmax'], 'L1_ffn_down_q': _L1_ffn_in['down_q'], 'L1_ffn_down_absmax': _L1_ffn_in['down_absmax']}
    _x0 = _d['L0_attn_x']
    _d['L0_attn_x'] = jax.random.normal(jax.random.fold_in(jax.random.key(seed), 1), (2, 1024, 512), dtype=_x0.dtype)
    del _x0
    return _d

def reference(L0_attn_x, L0_attn_w_qkv, L0_attn_w_o, L0_ffn_W_up, L0_ffn_gate_w, L0_ffn_expert_bias, L0_ffn_lora_A, L0_ffn_lora_B, L1_attn_Wq, L1_attn_Wk, L1_attn_Wv, L1_attn_Wo, L1_ffn_gate_q, L1_ffn_gate_absmax, L1_ffn_up_q, L1_ffn_up_absmax, L1_ffn_down_q, L1_ffn_down_absmax):

    def _L0_attn_ref(x, w_qkv, w_o):
        import jax, jax.numpy as jnp
        import numpy as np
        N_HEADS = 32
        N_KV_HEADS = 8
        DIM = 512
        HEAD_DIM = DIM // N_HEADS
        N_REP = N_HEADS // N_KV_HEADS
        ROPE_THETA = 10000.0

        def _apply_rope(x):
            seq = x.shape[2]
            hd = x.shape[-1]
            inv_freq = 1.0 / ROPE_THETA ** (jnp.arange(0, hd, 2, dtype=jnp.float32) / hd)
            angles = jnp.arange(seq, dtype=jnp.float32)[:, None] * inv_freq[None, :]
            cos = jnp.cos(angles)[None, None]
            sin = jnp.sin(angles)[None, None]
            x1 = x[..., 0::2]
            x2 = x[..., 1::2]
            r1 = x1 * cos - x2 * sin
            r2 = x1 * sin + x2 * cos
            return jnp.stack([r1, r2], axis=-1).reshape(x.shape)
        bs, seq, _ = x.shape
        qkv = x @ w_qkv
        q_sz = N_HEADS * HEAD_DIM
        kv_sz = N_KV_HEADS * HEAD_DIM
        xq = qkv[..., :q_sz].reshape(bs, seq, N_HEADS, HEAD_DIM).transpose(0, 2, 1, 3)
        xk = qkv[..., q_sz:q_sz + kv_sz].reshape(bs, seq, N_KV_HEADS, HEAD_DIM).transpose(0, 2, 1, 3)
        xv = qkv[..., q_sz + kv_sz:].reshape(bs, seq, N_KV_HEADS, HEAD_DIM).transpose(0, 2, 1, 3)
        xq = _apply_rope(xq)
        xk = _apply_rope(xk)
        keys = jnp.repeat(xk, N_REP, axis=1)
        values = jnp.repeat(xv, N_REP, axis=1)
        scale = 1.0 / jnp.sqrt(jnp.float32(HEAD_DIM))
        scores = jnp.einsum('bhsd,bhtd->bhst', xq, keys) * scale
        causal = jnp.tril(jnp.ones((seq, seq), dtype=bool))[None, None]
        scores = jnp.where(causal, scores, -jnp.inf)
        probs = jax.nn.softmax(scores, axis=-1)
        out = jnp.einsum('bhst,bhtd->bhsd', probs, values)
        out = out.transpose(0, 2, 1, 3).reshape(bs, seq, N_HEADS * HEAD_DIM)
        return out @ w_o

    def _L0_ffn_ref(x, W_up, gate_w, expert_bias, lora_A, lora_B):
        import jax, jax.numpy as jnp
        import numpy as np
        NUM_EXPERTS = 4
        HIDDEN = 512
        RANK = 8
        ALPHA = 8.0
        SCALE = ALPHA / RANK
        B, T, H = x.shape
        E = gate_w.shape[0]
        x_flat = x.reshape(-1, H)
        logits = x_flat @ gate_w.T + expert_bias
        top1 = jnp.argmax(logits, axis=-1)
        one_hot = jax.nn.one_hot(top1, E, dtype=x_flat.dtype)
        base_out = jnp.einsum('bth,oh->bto', x, W_up)
        z = jnp.einsum('nh,erh->ner', x_flat, lora_A)
        d = jnp.einsum('ner,ehr->neh', z, lora_B) * SCALE
        delta = jnp.einsum('neh,ne->nh', d, one_hot)
        return base_out + delta.reshape(B, T, H)

    def _L1_attn_ref(hidden_states, Wq, Wk, Wv, Wo):
        import jax, jax.numpy as jnp
        import numpy as np
        H = 32
        HKV = 8
        D = 512
        HD = D // H
        S = 128
        MASK_OUT = 0.9
        MIN_REMAIN = 128
        THETA = 10000.0

        def rope_tables(seq_len, hd):
            inv_freq = 1.0 / THETA ** (jnp.arange(0, hd, 2, dtype=jnp.float32) / hd)
            t = jnp.arange(seq_len, dtype=jnp.float32)
            freqs = jnp.outer(t, inv_freq)
            emb = jnp.concatenate([freqs, freqs], axis=-1)
            return (jnp.cos(emb), jnp.sin(emb))

        def rotate_half(x):
            x1, x2 = jnp.split(x, 2, axis=-1)
            return jnp.concatenate([-x2, x1], axis=-1)

        def apply_rope(x, cos, sin):
            return x * cos + rotate_half(x) * sin
        B, Sq, Dm = hidden_states.shape
        dtype = hidden_states.dtype
        neg = jnp.finfo(dtype).min
        q = (hidden_states @ Wq.T).reshape(B, Sq, H, HD).transpose(0, 2, 1, 3)
        k = (hidden_states @ Wk.T).reshape(B, Sq, HKV, HD).transpose(0, 2, 1, 3)
        v = (hidden_states @ Wv.T).reshape(B, Sq, HKV, HD).transpose(0, 2, 1, 3)
        rep = H // HKV
        k = jnp.repeat(k, rep, axis=1)
        v = jnp.repeat(v, rep, axis=1)
        cos, sin = rope_tables(Sq, HD)
        qr = apply_rope(q, cos, sin)
        kr = apply_rope(k, cos, sin)
        draft = jnp.einsum('bhqd,bhkd->bhqk', qr, kr)
        qi = jnp.arange(Sq)
        ki = jnp.arange(Sq)
        causal_future = qi[:, None] < ki[None, :]
        draft = draft + jnp.where(causal_future, neg, jnp.asarray(0.0, dtype))
        num_remain = max(min(Sq, MIN_REMAIN), Sq - int(Sq * MASK_OUT))
        _, draft_indices = jax.lax.top_k(draft, num_remain)
        mask = jnp.full((B, H, Sq, Sq), neg, dtype)
        b_idx = jnp.arange(B)[:, None, None, None]
        h_idx = jnp.arange(H)[None, :, None, None]
        s_idx = jnp.arange(Sq)[None, None, :, None]
        mask = mask.at[b_idx, h_idx, s_idx, draft_indices].set(0.0)
        mask = jnp.where(causal_future[None, None, :, :], neg, mask)
        scores = jnp.einsum('bhqd,bhkd->bhqk', qr, kr) / np.sqrt(HD).astype(np.float32) + mask
        attn = jax.nn.softmax(scores, axis=-1)
        out = jnp.einsum('bhqk,bhkd->bhqd', attn, v)
        out = out.transpose(0, 2, 1, 3).reshape(B, Sq, Dm)
        return out @ Wo.T

    def _L1_ffn_ref(x, gate_q, gate_absmax, up_q, up_absmax, down_q, down_absmax):
        import jax, jax.numpy as jnp
        import numpy as np
        BLOCK = 64
        NF4_CODE = jnp.array([-1.0, -0.6961928009986877, -0.5250730514526367, -0.39491748809814453, -0.28444138169288635, -0.18477343022823334, -0.09105003625154495, 0.0, 0.07958029955625534, 0.16093020141124725, 0.24611230194568634, 0.33791524171829224, 0.44070982933044434, 0.5626170039176941, 0.7229568362236023, 1.0], dtype=jnp.float32)

        def dequant_nf4(q, absmax, shape):
            w = NF4_CODE[q.reshape(-1)]
            w = w.reshape(-1, BLOCK) * absmax[:, None]
            return w.reshape(shape)
        HD = x.shape[-1]
        M = gate_q.shape[0]
        Wg = dequant_nf4(gate_q, gate_absmax, (M, HD))
        Wu = dequant_nf4(up_q, up_absmax, (M, HD))
        Wd = dequant_nf4(down_q, down_absmax, (HD, M))
        g = jnp.einsum('bsh,mh->bsm', x, Wg)
        u = jnp.einsum('bsh,mh->bsm', x, Wu)
        h = jax.nn.silu(g) * u
        return jnp.einsum('bsm,hm->bsh', h, Wd)
    x = L0_attn_x
    xn = _layernorm(x, axis=-1)
    x = x + _L0_attn_ref(xn, L0_attn_w_qkv, L0_attn_w_o) + _L0_ffn_ref(xn, L0_ffn_W_up, L0_ffn_gate_w, L0_ffn_expert_bias, L0_ffn_lora_A, L0_ffn_lora_B)
    xn = _layernorm(x, axis=-1)
    x = x + _L1_attn_ref(xn, L1_attn_Wq, L1_attn_Wk, L1_attn_Wv, L1_attn_Wo) + _L1_ffn_ref(xn, L1_ffn_gate_q, L1_ffn_gate_absmax, L1_ffn_up_q, L1_ffn_up_absmax, L1_ffn_down_q, L1_ffn_down_absmax)
    return x

_drawn_inputs = setup_inputs


def setup_inputs(seed=0):
    import zlib

    import numpy as np

    out = dict(_drawn_inputs(seed))
    spreads = {'L0_ffn_expert_bias': (0.0, 0.8)}
    factors = {'L0_attn_w_qkv': 4.79,
     'L0_attn_w_o': 4.596,
     'L0_ffn_gate_w': 3.43,
     'L0_ffn_lora_A': 2.962,
     'L0_ffn_lora_B': 2.942,
     'L1_attn_Wq': 4.896,
     'L1_attn_Wk': 4.914,
     'L1_attn_Wv': 3.362,
     'L1_attn_Wo': 3.416,
     'L1_ffn_gate_absmax': 4.48,
     'L1_ffn_up_absmax': 4.539,
     'L1_ffn_down_absmax': 4.529}
    for name, (base, spread) in spreads.items():
        noise = np.random.default_rng([zlib.crc32(name.encode()), seed]).standard_normal(out[name].shape)
        drawn = base * np.exp(spread * noise) if base else spread * noise
        out[name] = jnp.asarray(drawn.astype(out[name].dtype))
    for name, factor in factors.items():
        out[name] = (out[name] * factor).astype(out[name].dtype)
    return out
```

```python
from contextlib import ExitStack

import concourse.bass as bass
from concourse import mybir

F32 = mybir.dt.float32
BF16 = mybir.dt.bfloat16
I32 = mybir.dt.int32
ALU = mybir.AluOpType
ACT = mybir.ActivationFunctionType
AX = mybir.AxisListType

P = 128
T = 2048
D = 512
KC = D // P
NT = T // P
SEQ = 1024
NB = SEQ // P
H, KV, HD = 32, 8, 16
HALF = HD // 2
QK = (H + KV) * HD
QKV = QK + KV * HD
RB = QK // P
NE, NR = 4, 8
M = 1792
MC = M // P
TOP = 128
WINDOW = 8
WAVES = 32
NEG = -1.0e30
NTILE = 2 * NB
SCOL = [P * j * (j + 1) // 2 for j in range(NB + 1)]
TB = 4
TW = T // TB
DQ = M // 4
CREDIT = 64
POOL_JOINS = 4


def kernel_program(nc, poly, x, wqkv0, wo0, wup, gate_lora, expert_bias, lora_b, wqkv1, wo1,
                   gate_q, gate_am, up_q, up_am, down_q, down_am,
                   rope_cos, rope_sin, ident, causal, quantile, kappa, out):
    qkT = [nc.dram_tensor(f"qkT_{l}", [3, 2, QK, SEQ], BF16, kind="Internal").ap() for l in (0, 1)]
    v_d = [nc.dram_tensor(f"v_rows_{l}", [2, SEQ, KV * HD], F32, kind="Internal").ap() for l in (0, 1)]
    o_d = [nc.dram_tensor(f"attended_{l}", [WAVES, SEQ, 2 * HD], F32, kind="Internal").ap() for l in (0, 1)]
    xT_d = nc.dram_tensor("xT_rows", [P, KC, T], F32, kind="Internal").ap()
    w_d = nc.dram_tensor("gate_up_weights", [2, KC, P, M], F32, kind="Internal").ap()

    ctx = ExitStack()
    with ctx:
        sems = {}

        def sem(name):
            if name not in sems:
                sems[name] = ctx.enter_context(nc.semaphore(name))
            return sems[name]

        def sb(c, name, shape, dt=F32):
            return c.enter_context(nc.sbuf_tensor(name, shape, dt))

        resid = sb(ctx, "resid", [P, NT, D])
        identf = sb(ctx, "identf", [P, P])
        identb = sb(ctx, "identb", [P, P], BF16)
        causalf = sb(ctx, "causalf", [P, P])
        causalb = sb(ctx, "causalb", [P, P], BF16)
        banks = ctx.enter_context(nc.psum_tensor("banks", [P, 8, 512], F32))

        def need(eng, name, count):
            eng.wait_ge(sem(name), count + CREDIT)
            if eng is nc.sync or eng is nc.gpsimd:
                stand_alone(eng)

        def stand_alone(eng):
            eng.wait_ge(sem("started"), 1)

        def credit(eng, l, *names):
            for n in names:
                eng.sem_inc(sem(f"{n}_{l}"), CREDIT)

        def barrier(eng, n):
            own = "pool_phase_ended" if eng is nc.gpsimd else "phase_ended"
            eng.drain().then_inc(sem(own), 1)
            eng.wait_ge(sem("phase_ended"), 4 * n)
            if n >= POOL_JOINS:
                eng.wait_ge(sem("pool_phase_ended"), n - POOL_JOINS + 1)

        def token_tile(i):
            return resid[:, bass.ds(i, 1), :].rearrange("p a n -> p (a n)")

        def over_tiles(eng, body):
            for seq in range(2):
                with eng.Fori(0, NB // 2 - seq) as t:
                    for k in range(2):
                        body(t * 2 + (k + seq * NB), t * 2 + k, seq, k, False)
            for k in range(2):
                body(NT - 2 + k, NB - 2 + k, 1, k, k == 1)

        def over_waves(eng, wave):
            with eng.Fori(0, WAVES // 2 - 1) as t:
                for k in range(2):
                    wave(t * 2 + k, k, 2)
            wave(WAVES - 2, 0, 1)
            wave(WAVES - 1, 1, 0)

        def project_buffers(c, l):
            b = {}
            for k in range(2):
                if l == 0:
                    b["xin", k] = sb(c, f"xin{k}", [P, D])
                b["xn", k] = sb(c, f"xn{l}{k}", [P, D])
                b["xT", k] = sb(c, f"xT{l}{k}", [P, KC, P])
                b["st", k] = sb(c, f"st{l}{k}", [P, 6])
                b["mv", k] = sb(c, f"mv{l}{k}", [P, 2])
                b["sd", k] = sb(c, f"sd{l}{k}", [P, 1])
                b["rs", k] = sb(c, f"rs{l}{k}", [P, 1])
                b["r", k] = sb(c, f"r{l}{k}", [P, QK])
                b["parts", k] = sb(c, f"parts{l}{k}", [P, 3, RB, P], BF16)
                b["v", k] = sb(c, f"v{l}{k}", [P, KV * HD])
                b["zm", k] = sb(c, f"zm{l}{k}", [P, NE * NR])
                b["zT", k] = sb(c, f"zT{l}{k}", [NE * NR, P])
            for n in range(4):
                b["t", n] = sb(c, f"rope_t{l}{n}", [P, H + KV, HALF])
            b["d1"] = sb(c, f"d1{l}", [P, RB, P])
            b["wqkv"] = sb(c, f"wqkv{l}", [P, KC, QKV])
            b["cos"] = sb(c, f"cos{l}", [P, NB, HALF])
            b["sin"] = sb(c, f"sin{l}", [P, NB, HALF])
            b["eps"] = sb(c, f"eps{l}", [P, 1])
            if l == 0:
                b["wup"] = sb(c, "wup", [P, KC, D])
                b["gl"] = sb(c, "gl", [P, KC, NE + NE * NR])
                b["lb"] = sb(c, "lb", [NE * NR, D])
                b["bias"] = sb(c, "bias", [P, NE])
                b["rank"] = sb(c, "rank", [P, NE])
                for n in ("lg", "eq", "key", "oh"):
                    b[n] = sb(c, n, [P, NE])
                for n in ("mx", "mk"):
                    b[n] = sb(c, n, [P, 1])
            return b

        QKV_PS = banks[:, 0:2, :].rearrange("p a n -> p (a n)")
        UP_PS = banks[:, 2, :]
        TX_PS = banks[:, 3, :].rearrange("p (c n) -> p c n", c=KC)
        TR_PS = banks[:, 4:6, :].rearrange("p a n -> p (a n)")[:, 0:QK].rearrange("p (c n) -> p c n", c=RB)
        GL_PS = banks[:, 6, 0:NE + NE * NR]
        ZT_PS = banks[0:NE * NR, 7, 0:P]
        N_WEIGHTS = [9, 3]
        N_STORES = [4, 5]

        def slot_stores(l, i, k):
            return (i - k) * 8 * N_STORES[l]

        def project_sync(eng, l, b, wqkv):
            def s(n):
                return sem(f"{n}_{l}")
            loads = [(b["wqkv"][:, :, :], wqkv.rearrange("(c p) n -> p c n", p=P)),
                     (b["cos"][:, :, :], rope_cos.rearrange("(c p) n -> p c n", p=P)),
                     (b["sin"][:, :, :], rope_sin.rearrange("(c p) n -> p c n", p=P))]
            if l == 0:
                for k in range(2):
                    eng.dma_start(b["xin", k][:, :], x[k * P:(k + 1) * P, :]).then_inc(s(f"x_in{k}"), 16)
                loads += [(identf[:, :], ident), (causalf[:, :], causal),
                          (b["wup"][:, :, :], wup.rearrange("(c p) n -> p c n", p=P)),
                          (b["gl"][:, :, :], gate_lora.rearrange("(c p) n -> p c n", p=P)),
                          (b["lb"][:, :], lora_b),
                          (b["bias"][:, :], expert_bias.to_broadcast([P, NE]))]
            for dst, src in loads:
                eng.dma_start(dst, src).then_inc(s("weights_in"), 16)

            def body(i, pos, seq, k, last):
                need(eng, f"parts_ready_{l}", i + 1)
                for part in range(3):
                    dst = qkT[l][part, seq].rearrange("(c p) t -> p c t", p=P)
                    eng.dma_start(dst[:, :, bass.ts(pos, P)], b["parts", k][:, part]).then_inc(s(f"stored{k}"), 16)
                if l == 1:
                    need(eng, f"xT_ready_{l}", i + 1)
                need(eng, f"qkv_free_{l}", i + 1)
                eng.dma_start(v_d[l][seq][bass.ts(pos, P), :], b["v", k][:, :]).then_inc(s(f"stored{k}"), 16)
                if l == 1:
                    eng.dma_start(xT_d[:, :, bass.ts(i, P)], b["xT", k][:, :, :]).then_inc(s(f"stored{k}"), 16)
                elif not (isinstance(i, int)):
                    need(eng, "x_used_0", i + 1)
                    eng.dma_start(b["xin", k][:, :], x[bass.ts(i + 2, P), :]).then_inc(s(f"x_in{k}"), 16)
            over_tiles(eng, body)
            for k in range(2):
                eng.wait_ge(s(f"stored{k}"), slot_stores(l, NT + k, k))

        def project_tensor(pe, l, b):
            def transpose_x(i, k):
                need(pe, f"xn_ready_{l}", i + 1)
                for c in range(KC):
                    mm = nc.tensor.transpose(TX_PS[:, c, :], b["xn", k][:, c * P:(c + 1) * P], identf[:, :])
                mm.then_inc(sem(f"x_transposed_{l}"), 1)

            credit(pe, l, "x_transposed", "qkv_done", "gl_done", "r_transposed", "z_transposed", "up_done")
            pe.wait_ge(sem(f"weights_in_{l}"), 16 * N_WEIGHTS[l])
            transpose_x(0, 0)

            def body(i, pos, seq, k, last):
                need(pe, f"xT_ready_{l}", i + 1)
                need(pe, f"qkv_free_{l}", i)
                for lo, hi in ((0, 512), (512, QKV)):
                    for c in range(KC):
                        mm = nc.tensor.matmul(QKV_PS[:, lo:hi], b["xT", k][:, c, :], b["wqkv"][:, c, lo:hi],
                                              start=(c == 0), stop=(c == KC - 1))
                mm.then_inc(sem(f"qkv_done_{l}"), 1)
                if l == 0:
                    need(pe, "x_used_0", i)
                    for c in range(KC):
                        nc.tensor.matmul(UP_PS, b["xT", k][:, c, :], b["wup"][:, c, :], start=(c == 0), stop=False)
                    need(pe, "zm_ready_0", i)
                    for c in range(KC):
                        mm = nc.tensor.matmul(GL_PS, b["xT", k][:, c, :], b["gl"][:, c, :],
                                              start=(c == 0), stop=(c == KC - 1))
                    mm.then_inc(sem("gl_done_0"), 1)
                if not last:
                    transpose_x(i + 1, 1 - k)
                need(pe, f"r_ready_{l}", i + 1)
                need(pe, f"tr_free_{l}", i)
                for c in range(RB):
                    mm = nc.tensor.transpose(TR_PS[:, c, :], b["r", k][:, c * P:(c + 1) * P], identf[:, :])
                mm.then_inc(sem(f"r_transposed_{l}"), 1)
                if l == 0:
                    need(pe, "zm_ready_0", i + 1)
                    nc.tensor.transpose(ZT_PS, b["zm", k][:, :], identf[:, :]).then_inc(sem("z_transposed_0"), 1)
                    need(pe, "zT_ready_0", i + 1)
                    nc.tensor.matmul(UP_PS, b["zT", k][:, :], b["lb"][:, :], start=False,
                                     stop=True).then_inc(sem("up_done_0"), 1)
            over_tiles(pe, body)

        def project_scalar(act, l, b):
            def head(i, k):
                need(act, f"var_ready_{l}", i + 1)
                nc.scalar.activation(b["sd", k][:, :], b["mv", k][:, 1:2], ACT.Sqrt,
                                     bias=b["eps"][:, :]).then_inc(sem(f"sd_ready_{l}"), 1)

            def copy_x(i, k):
                need(act, f"x_transposed_{l}", i + 1)
                nc.scalar.activation(b["xT", k][:, :, :], TX_PS, ACT.Copy).then_inc(sem(f"xT_ready_{l}"), 1)

            credit(act, l, "sd_ready", "xT_ready", "part1_ready", "zT_ready")
            act.wait_ge(sem(f"consts_ready_{l}"), 1)
            head(0, 0)
            copy_x(0, 0)

            def body(i, pos, seq, k, last):
                if not last:
                    head(i + 1, 1 - k)
                    need(act, f"qkv_done_{l}" if l else "gl_done_0", i)
                    if l:
                        act.wait_ge(sem(f"stored{1 - k}_1"), slot_stores(l, i + 1, 1 - k))
                    copy_x(i + 1, 1 - k)
                need(act, f"r_transposed_{l}", i + 1)
                act.wait_ge(sem(f"stored{k}_{l}"), slot_stores(l, i, k))
                nc.scalar.activation(b["parts", k][:, 0], TR_PS, ACT.Copy).then_inc(sem(f"part1_ready_{l}"), 1)
                if l == 0:
                    need(act, "z_transposed_0", i + 1)
                    nc.scalar.activation(b["zT", k][:, :], ZT_PS, ACT.Copy).then_inc(sem("zT_ready_0"), 1)
            over_tiles(act, body)

        def project_vector(v, l, b):
            dve = nc.vector
            credit(v, l, "var_ready", "xn_ready", "qkv_free", "r_ready", "zm_ready", "tr_free",
                   "parts_ready", "x_used")
            dve.memset(b["eps"][:, :], 1e-5)
            if l == 0:
                for e in range(NE):
                    dve.memset(b["rank"][:, e:e + 1], float(NE - e))
            v.drain().then_inc(sem(f"consts_ready_{l}"), 1)
            v.wait_ge(sem(f"weights_in_{l}"), 16 * N_WEIGHTS[l])
            if l == 0:
                dve.tensor_copy(identb[:, :], identf[:, :])
                dve.tensor_copy(causalb[:, :], causalf[:, :])

            def norm(i, k):
                if l == 0:
                    src = b["xin", k][:, :]
                    v.wait_ge(sem(f"x_in{k}_0"), (i - k) * 8 + 16)
                else:
                    src = token_tile(i)
                dve.bn_stats(b["st", k][:, :], src)
                v.drain()
                dve.bn_aggr(b["mv", k][:, :], b["st", k][:, :])
                v.drain().then_inc(sem(f"var_ready_{l}"), 1)
                need(v, f"sd_ready_{l}", i + 1)
                dve.reciprocal(b["rs", k][:, :], b["sd", k][:, :])
                v.drain()
                need(v, f"x_transposed_{l}", i - 1)
                dve.tensor_scalar(b["xn", k][:, :], src, b["mv", k][:, 0:1], b["rs", k][:, :],
                                  ALU.subtract, ALU.mult).then_inc(sem(f"xn_ready_{l}"), 1)

            norm(0, 0)

            def body(i, pos, seq, k, last):
                if not last:
                    norm(i + 1, 1 - k)
                need(v, f"qkv_done_{l}", i + 1)
                if l == 0:
                    hv = QKV_PS[:, 0:QK].rearrange("p (h i two) -> p h two i", h=H + KV, two=2)
                else:
                    hv = QKV_PS[:, 0:QK].rearrange("p (h two i) -> p h two i", h=H + KV, two=2)
                x1, x2 = hv[:, :, 0, :], hv[:, :, 1, :]
                cos = b["cos"][:, bass.ds(pos, 1), :].to_broadcast([P, H + KV, HALF])
                sin = b["sin"][:, bass.ds(pos, 1), :].to_broadcast([P, H + KV, HALF])
                for n, (src, tab) in enumerate(((x1, cos), (x2, sin), (x1, sin), (x2, cos))):
                    dve.tensor_tensor(b["t", n][:, :, :], src, tab, ALU.mult)
                v.wait_ge(sem(f"stored{k}_{l}"), slot_stores(l, i, k))
                dve.tensor_copy(b["v", k][:, :], QKV_PS[:, QK:QKV])
                v.drain().then_inc(sem(f"qkv_free_{l}"), 1)
                need(v, f"r_transposed_{l}", i - 1)
                rv = b["r", k][:, :].rearrange("p (h two i) -> p h two i", h=H + KV, two=2)
                dve.tensor_tensor(rv[:, :, 0, :], b["t", 0][:, :, :], b["t", 1][:, :, :], ALU.subtract)
                dve.tensor_tensor(rv[:, :, 1, :], b["t", 2][:, :, :], b["t", 3][:, :, :], ALU.add)
                v.drain().then_inc(sem(f"r_ready_{l}"), 1)
                if l == 0:
                    need(v, "gl_done_0", i + 1)
                    dve.tensor_tensor(b["lg"][:, :], GL_PS[:, 0:NE], b["bias"][:, :], ALU.add)
                    v.drain()
                    dve.tensor_reduce(b["mx"][:, :], b["lg"][:, :], AX.X, ALU.max)
                    v.drain()
                    dve.tensor_scalar(b["eq"][:, :], b["lg"][:, :], b["mx"][:, :], None, ALU.is_ge)
                    v.drain()
                    dve.tensor_tensor(b["key"][:, :], b["eq"][:, :], b["rank"][:, :], ALU.mult)
                    v.drain()
                    dve.tensor_reduce(b["mk"][:, :], b["key"][:, :], AX.X, ALU.max)
                    v.drain()
                    dve.tensor_scalar(b["oh"][:, :], b["key"][:, :], b["mk"][:, :], None, ALU.is_equal)
                    v.drain()
                    need(v, "z_transposed_0", i - 1)
                    dve.tensor_tensor(b["zm", k][:, :].rearrange("p (e r) -> p e r", e=NE),
                                      GL_PS[:, NE:].rearrange("p (e r) -> p e r", e=NE),
                                      b["oh"][:, :].rearrange("p (e a) -> p e a", a=1).to_broadcast([P, NE, NR]),
                                      ALU.mult).then_inc(sem("zm_ready_0"), 1)
                need(v, f"part1_ready_{l}", i + 1)
                dve.tensor_tensor(b["d1"][:, :, :], TR_PS, b["parts", k][:, 0], ALU.subtract)
                v.drain().then_inc(sem(f"tr_free_{l}"), 1)
                dve.tensor_copy(b["parts", k][:, 1], b["d1"][:, :, :])
                v.drain()
                dve.tensor_tensor(b["parts", k][:, 2], b["d1"][:, :, :], b["parts", k][:, 1], ALU.subtract)
                v.drain().then_inc(sem(f"parts_ready_{l}"), 1)
                if l == 0:
                    need(v, "up_done_0", i + 1)
                    dve.tensor_tensor(token_tile(i), UP_PS, b["xin", k][:, :], ALU.add)
                    v.drain().then_inc(sem("x_used_0"), 1)
            over_tiles(v, body)

        def dequantise(eng, e, q, am, res, sign, mag, acc):
            def op(*a):
                e.tensor_scalar(*a)
                eng.drain()

            def op2(*a):
                e.tensor_tensor(*a)
                eng.drain()
            op(mag, q, 1.0, -7.5, ALU.mult, ALU.add)
            op(sign, mag, 2.0, 1.0, ALU.mult, ALU.mult)
            op(sign, sign, 1.0, -1.0, ALU.min, ALU.max)
            op2(mag, mag, sign, ALU.mult)
            op(mag, mag, 1.0, -4.0, ALU.mult, ALU.add)
            for y, co in ((acc, poly[0]), (res, poly[1])):
                op(y, mag, co[0], co[1], ALU.mult, ALU.add)
                for c in co[2:]:
                    op2(y, y, mag, ALU.mult)
                    op(y, y, 1.0, c, ALU.mult, ALU.add)
            op2(acc, acc, sign, ALU.mult)
            op2(res, res, acc, ALU.add)
            op2(res, res, am, ALU.mult)

        def dequantise_gate_up(pool, b):
            nc.gpsimd.memset(b["token"][:, :], 0.0)
            pool.drain()
            for m, (q_d, am_d) in enumerate(((gate_q, gate_am), (up_q, up_am))):
                with pool.Fori(0, KC) as c:
                    for u in range(4):
                        k, n = u % 2, (c + m * KC) * 2 + u // 2
                        cols = slice(u * DQ, (u + 1) * DQ)
                        pool.dma_start(b["q", k][:, :], q_d[bass.ts(c, P), cols]).then_inc(sem(f"dq_in{k}"), 16)
                        for h in range(2):
                            pool.dma_start(b["am", k][64 * h:64 * h + 64, :],
                                           am_d[bass.ds(c * 2 + h, 1), cols].to_broadcast([64, DQ])
                                           ).then_inc(sem(f"dq_in{k}"), 16)
                        pool.wait_ge(sem(f"dq_in{k}"), (n + 1) * 48)
                        pool.wait_ge(sem(f"dq_out{k}"), n * 16)
                        nc.gpsimd.tensor_tensor(b["token"][:, :], b["token"][:, :], b["token"][:, :], ALU.mult)
                        dequantise(pool, nc.gpsimd, b["q", k][:, :], b["am", k][:, :], b["res", k][:, :],
                                   b["sign"][:, :], b["mag"][:, :], b["acc"][:, :])
                        pool.dma_start(w_d[m][bass.ds(c, 1), :, cols].rearrange("a p n -> (a p) n"),
                                       b["res", k][:, :]).then_inc(sem(f"dq_out{k}"), 16)
            for k in range(2):
                pool.wait_ge(sem(f"dq_out{k}"), 16 * 4 * KC)

        def attend_buffers(c, l):
            b = {}
            for k in range(2):
                b["K", k] = sb(c, f"K{l}{k}", [P, SEQ], BF16)
                b["Q", k] = sb(c, f"Q{l}{k}", [P, 2, SEQ], BF16)
                b["V", k] = sb(c, f"V{l}{k}", [P, NB, 32])
                b["O", k] = sb(c, f"O{l}{k}", [P, NB, 2 * HD])
                b["OT", k] = sb(c, f"OT{l}{k}", [P, 4, P])
                b["sum", k] = sb(c, f"sum{l}{k}", [P, 2, NB])
                b["rsum", k] = sb(c, f"rsum{l}{k}", [P, 2, NB])
                b["PT", k] = sb(c, f"PT{l}{k}", [P, NB, P])
                b["nmax", k] = sb(c, f"nmax{l}{k}", [P, 2, NB])
                b["P", k] = sb(c, f"P{l}{k}", [P, SEQ])
            b["zeroV"] = sb(c, f"zeroV{l}", [P, 32])
            b["red"] = sb(c, f"red{l}", [P, 4, HD])
            if l == 1:
                for k in range(2):
                    b["S", k] = sb(c, f"S{k}", [P, 2, SCOL[NB]])
                    for n in STATE:
                        b[n, k] = sb(c, f"{n}{k}", [P, 2, NB])
                    b["junk", k] = sb(c, f"junk{k}", [P, SEQ], BF16)
                for n in ("p1", "p2", "p3", "p4", "p5", "v1", "v2", "v3", "v4", "v5", "theta", "half", "minus", "cols"):
                    b[n] = sb(c, n, [P, 2, NB])
                for k in range(3):
                    b["E", k] = sb(c, f"E{k}", [P, SEQ])
                    b["Y", k] = sb(c, f"Y{k}", [P, SEQ])
                b["top8"] = sb(c, "top8", [P, 2, NB, 8])
                b["pick"] = sb(c, "pick", [P, 2, NB, 8])
                b["iota8"] = sb(c, "iota8", [P, 8])
                b["quant"] = sb(c, "quant", [P, NB])
                b["kappa"] = sb(c, "kappa", [P, NB])
            return b

        STATE = ("max", "ssq", "t", "nt", "cnt", "lo", "clo", "hi", "chi", "kap", "blo", "bhi")

        def width(j):
            return P * (j + 1)

        def s_ps(n):
            return banks[:, 2 * (n % 2):2 * (n % 2) + 2, :].rearrange("p a n -> p (a n)")

        def pt_ps(m):
            return banks[:, 4 + m % 2, :].rearrange("p (c q) -> p c q", c=4)

        OT_PS = banks[:, 6, :].rearrange("p (a q) -> p a q", a=4)
        OQ_PS = banks[:, 7, :].rearrange("p (a c d) -> p a c d", a=4, c=4)
        HALVES = [1 if j < 4 else 2 for j in range(NB)]
        PT_AT = [sum((HALVES * 2)[:n]) for n in range(NTILE + 1)]
        PT_WAVE = PT_AT[NTILE]

        def attend_sync(eng, l, b):
            def s(n):
                return sem(f"{n}_{l}")
            if l == 1:
                eng.dma_start(b["quant"][:, :], quantile).then_inc(sem("tables_in"), 16)
                eng.dma_start(b["kappa"][:, :], kappa).then_inc(sem("tables_in"), 16)
            with eng.Fori(0, 2) as q:
                with eng.Fori(0, KV) as g:
                    for k in range(2):
                        w = (q * KV + g) * 2 + k
                        need(eng, f"s_done_{l}", (w - 1) * NTILE)
                        for part in range(3):
                            rows = qkT[l][part][bass.ds(q, 1)].rearrange("a r t -> (a r) t")
                            kr = rows[bass.ds(g * HD + H * HD, HD), :]
                            qr = rows[bass.ds(g * 4 * HD + k * 2 * HD, 2 * HD), :].rearrange("(h d) t -> d h t", d=HD)
                            for rep in range(3 if part < 2 else 2):
                                at = (3 * part + rep) * HD
                                eng.dma_start(b["Q", k][at:at + HD, :, :], qr).then_inc(s(f"qk_in{k}"), 16)
                                at = (part + 3 * rep) * HD
                                eng.dma_start(b["K", k][at:at + HD, :], kr).then_inc(s(f"qk_in{k}"), 16)
                        need(eng, f"value_done_{l}", (w - 1) * NTILE)
                        vr = v_d[l][bass.ds(q, 1)].rearrange("a (c p) d -> (a p) c d", p=P)
                        eng.dma_start(b["V", k][:, :, 0:HD], vr[:, :, bass.ds(g * HD, HD)]).then_inc(s(f"v_in{k}"), 16)
            for k in range(2):
                eng.wait_ge(s(f"o_out{k}"), 16 * WAVES // 2)

        def attend_tensor(pe, l, b):
            def scores(n, k, w):
                r, j = divmod(n, NB)
                if n == 0:
                    pe.wait_ge(sem(f"qk_in{k}_{l}"), (w - k + 2) * 128)
                ps = s_ps(n)
                need(pe, ("p_ready_0", "s_stored_1")[l], w * NTILE + (n - 1))
                for lo in range(0, width(j), 512):
                    hi = min(lo + 512, width(j))
                    nc.tensor.matmul(ps[:, lo:hi], b["Q", k][:, r, j * P:(j + 1) * P], b["K", k][:, lo:hi],
                                     start=True, stop=(hi != width(j)))
                nc.tensor.matmul(ps[:, j * P:(j + 1) * P], identb[:, :], causalb[:, :],
                                 start=False, stop=True).then_inc(sem(f"s_done_{l}"), 1)

            def turn(n, k, w):
                need(pe, f"p_ready_{l}", w * NTILE + (n + 1))
                j = n % NB
                for h in range(HALVES[j]):
                    m = PT_AT[n] + h
                    need(pe, f"pt_used{m % 2}_{l}", w * (PT_WAVE // 2) + m // 2)
                    for c in range(min(4, j + 1 - 4 * h)):
                        at = (4 * h + c) * P
                        mm = nc.tensor.transpose(pt_ps(m)[:, c, :], b["P", n % 2][:, at:at + P], identf[:, :])
                    mm.then_inc(sem(f"turned_{l}"), 1)

            def values(n, k, w):
                j = n % NB
                if n == 0:
                    pe.wait_ge(sem(f"v_in{k}_{l}"), (w - k + 2) * 8)
                need(pe, f"pt_used0_{l}", w * (PT_WAVE // 2) + (PT_AT[n + 1] + 1) // 2)
                need(pe, f"pt_used1_{l}", w * (PT_WAVE // 2) + PT_AT[n + 1] // 2)
                if n % 4 == 0:
                    need(pe, f"ot_copied_{l}", w * 4 + n // 4)
                for g in range(j + 1, 4):
                    nc.tensor.matmul(OT_PS[32 * g:32 * g + 32, j % 4, :], b["zeroV"][:, :], b["PT", n % 2][:, 0, :],
                                     start=True, stop=True)
                for c in range(j + 1):
                    g = c % 4
                    mm = nc.tensor.matmul(OT_PS[32 * g:32 * g + 32, j % 4, :], b["V", k][:, c, :],
                                          b["PT", n % 2][:, c, :], start=(c < 4), stop=(c + 4 > j))
                mm.then_inc(sem(f"value_done_{l}"), 1)

            def rows(m, w):
                need(pe, f"ot_copied_{l}", w * 4 + (m + 1))
                need(pe, f"oq_read_{l}", w * 4 + m)
                for a in range(4):
                    mm = nc.tensor.transpose(banks[:, 7, a * P:(a + 1) * P], b["OT", m % 2][:, a, :], identf[:, :])
                mm.then_inc(sem(f"rows_done_{l}"), 1)

            def wave(w, k, left):
                if l == 1 and left == 2:
                    for n in range(2):
                        scores(n, k, w + 2)
                for n in range(NTILE):
                    if l == 0 and n + 2 < NTILE:
                        scores(n + 2, k, w)
                    elif l == 0 and left:
                        scores(n + 2 - NTILE, 1 - k, w + 1)
                    turn(n, k, w)
                    if n > 0:
                        values(n - 1, k, w)
                    if n % 4 == 1 and n > 1:
                        rows(n // 4 - 1, w)
                values(NTILE - 1, k, w)
                rows(3, w)
                if l == 1 and left == 2:
                    for n in range(2, NTILE):
                        scores(n, k, w + 2)

            credit(pe, l, "s_done", "turned", "value_done", "rows_done")
            pe.wait_ge(sem(f"att_consts_{l}"), 1)
            if l == 0:
                for n in range(2):
                    scores(n, 0, 0)
            else:
                for w in range(2):
                    for n in range(NTILE):
                        scores(n, w, w)
            over_waves(pe, wave)

        def pt_copy(eng, copy, l, b, n, w, h):
            m = PT_AT[n] + h
            blocks = min(4, n % NB + 1 - 4 * h)
            need(eng, f"turned_{l}", w * PT_WAVE + (m + 1))
            need(eng, f"value_done_{l}", w * NTILE + (n - 1))
            copy(b["PT", n % 2][:, 4 * h:4 * h + blocks, :], pt_ps(m)[:, 0:blocks, :]).then_inc(
                sem(f"pt_used{m % 2}_{l}"), 1)

        def attend_scalar(act, l, b):
            def copy(dst, src):
                return nc.scalar.activation(dst, src, ACT.Copy)

            def ot_copy(m, w):
                need(act, f"value_done_{l}", w * NTILE + (4 * m + 4))
                need(act, f"rows_done_{l}", w * 4 + (m - 1))
                copy(b["OT", m % 2][:, :, :], OT_PS).then_inc(sem(f"ot_copied_{l}"), 1)

            def store(k, w):
                need(act, f"o_ready_{l}", w * 4 + 4)
                act.dma_start(o_d[l][bass.ds(w, 1)].rearrange("a (c p) d -> (a p) c d", p=P),
                              b["O", k][:, :, :]).then_inc(sem(f"o_out{k}_{l}"), 16)

            def exp0(n, k, w):
                r, j = divmod(n, NB)
                need(act, "max_ready_0", w * NTILE + (n + 1))
                before = PT_AT[n - 1] if n >= 2 else PT_AT[n + NTILE - 1] - PT_WAVE
                need(act, "turned_0", w * PT_WAVE + before)
                nc.scalar.activation(b["P", n % 2][:, 0:width(j)], s_ps(n)[:, 0:width(j)], ACT.Exp,
                                     bias=b["nmax", k][:, r, j:j + 1],
                                     accum_out=b["sum", k][:, r, j:j + 1]).then_inc(sem("p_ready_0"), 1)

            def wave0(w, k, left):
                for n in range(NTILE):
                    if n + 1 < NTILE:
                        exp0(n + 1, k, w)
                    elif left:
                        exp0(0, 1 - k, w + 1)
                    if HALVES[n % NB] == 2:
                        pt_copy(act, copy, l, b, n, w, 1)
                    if n % 4 == 0 and n > 0:
                        ot_copy(n // 4 - 1, w)
                ot_copy(3, w)
                store(k, w)

            NJ = NB - 1
            PASS = 2 * NJ

            def square(k, w):
                for r in range(2):
                    for j in range(1, NB):
                        need(act, "s_stored_1", w * NTILE + (r * NB + j + 1))
                        one(k, w, 0, r, j, ACT.Square, j * P, "ssq", None)

            def one(k, w, p, r, j, func, cols, result, bias):
                n = p * PASS + r * NJ + j - 1
                need(act, "act_pass_1", w * (4 * PASS) + (n - 1))
                x = SCOL[j]
                more = {"bias": bias} if bias is not None else {}
                nc.scalar.activation(b["junk", n % 2][:, 0:cols], b["S", k][:, r, x:x + cols], func,
                                     accum_out=b[result, k][:, r, j:j + 1], **more).then_inc(sem("act_pass_1"), 1)

            def signs(k, w, rnd):
                for r in range(2):
                    need(act, "t_ready_1", (w * 3 + rnd) * 2 + (r + 1))
                    for j in range(1, NB):
                        one(k, w, rnd + 1, r, j, ACT.Sign, width(j), "cnt", b["nt", k][:, r, j:j + 1])

            def exp1(n, k, w):
                r, j = divmod(n, NB)
                need(act, "max_ready_1", w + 1)
                need(act, "p_ready_1", w * NTILE + (n - 2))
                x = SCOL[j]
                nc.scalar.activation(b["E", n % 3][:, 0:width(j)], b["S", k][:, r, x:x + width(j)], ACT.Exp,
                                     bias=b["nmax", k][:, r, j:j + 1]).then_inc(sem("e_ready_1"), 1)

            def wave1(w, k, left):
                if left:
                    square(1 - k, w + 1)
                    signs(1 - k, w + 1, 0)
                    signs(1 - k, w + 1, 1)
                exp1(0, k, w)
                exp1(1, k, w)
                for n in range(NTILE):
                    if n + 2 < NTILE:
                        exp1(n + 2, k, w)
                    for h in range(HALVES[n % NB]):
                        pt_copy(act, copy, l, b, n, w, h)
                    if n % 4 == 0 and n > 0:
                        ot_copy(n // 4 - 1, w)
                ot_copy(3, w)
                if left:
                    signs(1 - k, w + 1, 2)
                store(k, w)

            act.wait_ge(sem(f"att_consts_{l}"), 1)
            if l == 0:
                credit(act, l, "p_ready", "pt_used1", "ot_copied")
                exp0(0, 0, 0)
                over_waves(act, wave0)
            else:
                credit(act, l, "pt_used0", "pt_used1", "ot_copied", "act_pass", "e_ready")
                square(0, 0)
                for rnd in range(3):
                    signs(0, 0, rnd)
                over_waves(act, wave1)

        def bracket(eng, e, b, tmp, k, rs, from_sign):
            target = TOP - 4.0
            u1, u2, u3, u4, u5 = (b[f"{tmp}{n}"][:, rs, 1:NB] for n in range(1, 6))
            c = {n: b[n, k][:, rs, 1:NB] for n in STATE}

            def ts(*a):
                e.tensor_scalar(*a)
                eng.drain()

            def tt(*a):
                e.tensor_tensor(*a)
                eng.drain()
            if from_sign:
                tt(c["cnt"], c["cnt"], b["cols"][:, rs, 1:NB], ALU.add)
                tt(c["cnt"], c["cnt"], b["half"][:, rs, 1:NB], ALU.mult)
            e.tensor_scalar(u1, c["cnt"], TOP + 0.25, None, ALU.is_gt)
            e.tensor_scalar(u2, c["cnt"], TOP - WINDOW - 0.25, None, ALU.is_lt)
            eng.drain()
            for flag, end, count, met in ((u1, "lo", "clo", "blo"), (u2, "hi", "chi", "bhi")):
                tt(c[met], c[met], flag, ALU.add)
                for dst, src in ((c[end], c["t"]), (c[count], c["cnt"])):
                    tt(u3, src, dst, ALU.subtract)
                    tt(u3, u3, flag, ALU.mult)
                    tt(dst, dst, u3, ALU.add)
            tt(u1, u1, u2, ALU.add)
            tt(u2, c["clo"], c["chi"], ALU.subtract)
            ts(u2, u2, 1.0, None, ALU.max)
            tt(u3, c["hi"], c["lo"], ALU.subtract)
            ts(u4, c["clo"], -target, None, ALU.add)
            tt(u3, u3, u4, ALU.mult)
            if from_sign:
                tt(u2, u2, b["minus"][:, rs, 1:NB], ALU.pow)
            else:
                e.reciprocal(u2, u2)
                eng.drain()
            tt(u3, u3, u2, ALU.mult)
            tt(u3, u3, c["lo"], ALU.add)
            ts(u4, c["cnt"], -target, None, ALU.add)
            tt(u4, u4, c["kap"], ALU.mult)
            tt(u4, u4, c["t"], ALU.add)
            tt(u3, u3, u4, ALU.subtract)
            tt(u5, c["blo"], c["bhi"], ALU.mult)
            ts(u5, u5, 1.0, None, ALU.min)
            tt(u3, u3, u5, ALU.mult)
            tt(u4, u4, u3, ALU.add)
            tt(u4, u4, c["t"], ALU.subtract)
            tt(u4, u4, u1, ALU.mult)
            tt(c["t"], c["t"], u4, ALU.add)
            ts(c["nt"], c["t"], -1.0, None, ALU.mult)

        def attend_gpsimd(pool, b):
            g = nc.gpsimd
            PASS = 2 * (NB - 1)
            credit(pool, 1, "t_ready", "t4_ready")
            g.memset(b["half"][:, :, :], 0.5)
            g.memset(b["minus"][:, :, :], -1.0)
            for j in range(1, NB):
                g.memset(b["cols"][:, :, j:j + 1], float(width(j)))
            pool.drain()
            pool.wait_ge(sem("att_consts_1"), 1)
            pool.wait_ge(sem("tables_in"), 32)

            def wave(w, k, left):
                for r in range(2):
                    rs = slice(r, r + 1)
                    need(pool, "act_pass_1", w * (4 * PASS) + (r + 1) * (NB - 1))
                    u1 = b["p1"][:, rs, 1:NB]
                    g.tensor_tensor(u1, b["ssq", k][:, rs, 1:NB], b["half"][:, rs, 1:NB], ALU.pow)
                    for n in ("blo", "bhi", "lo", "hi", "clo", "chi"):
                        g.memset(b[n, k][:, rs, 1:NB], 0.0)
                    pool.drain()
                    for name, tab in (("t", "quant"), ("kap", "kappa")):
                        g.tensor_tensor(b[name, k][:, rs, 1:NB], u1,
                                        b[tab][:, 1:NB].rearrange("p (a n) -> p a n", a=1), ALU.mult)
                    pool.drain()
                    g.tensor_scalar(b["nt", k][:, rs, 1:NB], b["t", k][:, rs, 1:NB], -1.0, None, ALU.mult)
                    pool.drain()
                    pool.sem_inc(sem("t_ready_1"), 1)
                for rnd in range(3):
                    for r in range(2):
                        need(pool, "act_pass_1", w * (4 * PASS) + (rnd + 1) * PASS + (r + 1) * (NB - 1))
                        bracket(pool, g, b, "p", k, slice(r, r + 1), True)
                        if rnd < 2:
                            pool.sem_inc(sem("t_ready_1"), 1)
                        else:
                            pool.sem_inc(sem("t4_ready_1"), 1)
            with pool.Fori(0, WAVES // 2) as t:
                for k in range(2):
                    wave(t * 2 + k, k, None)

        def attend_vector(v, l, b):
            dve = nc.vector

            def out_rows(m, k, w):
                r, j0 = (4 * m) // NB, (4 * m) % NB
                need(v, f"rows_done_{l}", w * 4 + (m + 1))
                if l == 0:
                    need(v, "p_ready_0", w * NTILE + (4 * m + 4))
                dve.tensor_reduce(b["red"][:, :, :], OQ_PS[:, :, :, 0:HD].rearrange("p a c d -> p a d c"), AX.X, ALU.add)
                dve.reciprocal(b["rsum", k][:, r, j0:j0 + 4], b["sum", k][:, r, j0:j0 + 4])
                v.drain().then_inc(sem(f"oq_read_{l}"), 1)
                if m == 0:
                    v.wait_ge(sem(f"o_out{k}_{l}"), (w - k) * 8)
                dve.tensor_tensor(b["O", k][:, j0:j0 + 4, r * HD:(r + 1) * HD], b["red"][:, :, :],
                                  b["rsum", k][:, r, j0:j0 + 4].rearrange("p (a o) -> p a o", o=1).to_broadcast([P, 4, HD]),
                                  ALU.mult)
                v.drain().then_inc(sem(f"o_ready_{l}"), 1)

            for k in range(2):
                dve.memset(b["V", k][:, :, HD:32], 0.0)
            dve.memset(b["zeroV"][:, :], 0.0)
            if l == 0:
                credit(v, l, "max_ready", "oq_read", "o_ready", "pt_used0")
                v.drain().then_inc(sem("att_consts_0"), 1)

                def maxes(n, k, w):
                    r, j = divmod(n, NB)
                    need(v, "s_done_0", w * NTILE + (n + 1))
                    dve.tensor_reduce(b["nmax", k][:, r, j:j + 1], s_ps(n)[:, 0:width(j)], AX.X, ALU.max,
                                      negate=True).then_inc(sem("max_ready_0"), 1)

                def wave0(w, k, left):
                    for n in range(NTILE):
                        if n + 2 < NTILE:
                            maxes(n + 2, k, w)
                        elif left:
                            maxes(n + 2 - NTILE, 1 - k, w + 1)
                        pt_copy(v, dve.tensor_copy, l, b, n, w, 0)
                        if n % 4 == 1 and n > 1:
                            out_rows(n // 4 - 1, k, w)
                    out_rows(3, k, w)
                for n in range(2):
                    maxes(n, 0, 0)
                over_waves(v, wave0)
                return

            credit(v, l, "s_stored", "max_ready", "p_ready", "oq_read", "o_ready")
            for e in range(8):
                dve.memset(b["iota8"][:, e:e + 1], float(e))
            dve.memset(b["theta"][:, :, :], NEG / 10)
            v.drain().then_inc(sem("att_consts_1"), 1)

            def store_scores(n, k, w):
                r, j = divmod(n, NB)
                x = SCOL[j]
                need(v, "s_done_1", w * NTILE + (n + 1))
                dve.tensor_scalar(b["S", k][:, r, x:x + width(j)], s_ps(n)[:, 0:width(j)], 1.0, None, ALU.mult,
                                  ALU.max, accum_out=b["max", k][:, r, j:j + 1]).then_inc(sem("s_stored_1"), 1)

            def end_store(k):
                v.drain()
                dve.tensor_scalar(b["nmax", k][:, :, :], b["max", k][:, :, :], -1.0, None, ALU.mult)
                v.drain().then_inc(sem("max_ready_1"), 1)

            def window(k, w):
                tiles = [(r, j) for r in range(2) for j in range(1, NB)]
                for n in range(len(tiles) + 2):
                    v.drain()
                    for stage in range(3):
                        q = n - stage
                        if not 0 <= q < len(tiles):
                            continue
                        r, j = tiles[q]
                        y = b["Y", q % 3][:, 0:width(j)]
                        sc = b["S", k][:, r, SCOL[j]:SCOL[j] + width(j)]
                        if stage == 0:
                            dve.tensor_scalar(y, sc, b["t", k][:, r, j:j + 1], None, ALU.is_ge, ALU.add,
                                              accum_out=b["cnt", k][:, r, j:j + 1])
                        elif stage == 1:
                            dve.scalar_tensor_tensor(y, y, NEG, sc, ALU.mult, ALU.add)
                        else:
                            dve.max(b["top8"][:, r, j, :], y)
                v.drain()

            def choose(k):
                c = {n: b[n, k][:, :, 1:NB] for n in STATE}
                u1, u2 = b["v1"][:, :, 1:NB], b["v2"][:, :, 1:NB]
                th = b["theta"][:, :, 1:NB]
                pick, top = b["pick"], b["top8"]
                dve.tensor_scalar(u1, c["cnt"], -1.0, TOP - 1.0, ALU.mult, ALU.add)
                dve.tensor_scalar(u2, c["cnt"], float(TOP), None, ALU.is_equal)
                v.drain()
                for r in range(2):
                    dve.tensor_tensor(pick[:, r, 1:NB, :],
                                      b["iota8"][:, :].rearrange("p (a n) -> p a n", a=1).to_broadcast([P, NB - 1, 8]),
                                      b["v1"][:, r, 1:NB].rearrange("p (a n) -> p a n", n=1).to_broadcast([P, NB - 1, 8]),
                                      ALU.is_equal)
                dve.tensor_tensor(u2, u2, c["t"], ALU.mult)
                v.drain()
                for r in range(2):
                    dve.tensor_tensor(pick[:, r, 1:NB, :], pick[:, r, 1:NB, :], top[:, r, 1:NB, :], ALU.mult)
                v.drain()
                for r in range(2):
                    dve.tensor_reduce(b["theta"][:, r, 1:NB], pick[:, r, 1:NB, :], AX.X, ALU.add)
                v.drain()
                dve.tensor_tensor(th, th, u2, ALU.add)
                v.drain()

            def count4(k, w):
                need(v, "t4_ready_1", 0)
                for r in range(2):
                    v.wait_ge(sem("t4_ready_1"), CREDIT + w * 2 + (r + 1))
                    for j in range(1, NB):
                        x = SCOL[j]
                        q = r * (NB - 1) + j - 1
                        if q % 3 == 0 and q:
                            v.drain()
                        dve.tensor_scalar(b["Y", q % 3][:, 0:width(j)], b["S", k][:, r, x:x + width(j)],
                                          b["t", k][:, r, j:j + 1], None, ALU.is_ge, ALU.add,
                                          accum_out=b["cnt", k][:, r, j:j + 1])
                v.drain()
                bracket(v, dve, b, "v", k, slice(0, 2), False)

            def products(k, w):
                for n in range(NTILE):
                    r, j = divmod(n, NB)
                    x = SCOL[j]
                    need(v, "e_ready_1", w * NTILE + (n + 1))
                    before = PT_AT[n - 1] if n >= 2 else PT_AT[n + NTILE - 1] - PT_WAVE
                    need(v, "turned_1", w * PT_WAVE + before)
                    dve.scalar_tensor_tensor(b["P", n % 2][:, 0:width(j)], b["S", k][:, r, x:x + width(j)],
                                             b["theta"][:, r, j:j + 1], b["E", n % 3][:, 0:width(j)],
                                             ALU.is_ge, ALU.mult,
                                             accum_out=b["sum", k][:, r, j:j + 1]).then_inc(sem("p_ready_1"), 1)
                    if n % 4 == 2 and n > 2:
                        out_rows(n // 4 - 1, k, w)

            def wave1(w, k, left):
                count4(k, w)
                window(k, w)
                choose(k)
                products(k, w)
                out_rows(3, k, w)
                if left == 2:
                    for n in range(NTILE):
                        store_scores(n, k, w + 2)
                    end_store(k)

            for w in range(2):
                for n in range(NTILE):
                    store_scores(n, w, w)
                end_store(w)
            over_waves(v, wave1)

        def output_buffers(c, l):
            b = {}
            for k in range(2):
                b["o", k] = sb(c, f"o{l}{k}", [P, D])
                b["oT", k] = sb(c, f"oT{l}{k}", [P, KC, P])
                b["res", k] = sb(c, f"res{l}{k}", [P, D])
            b["wo"] = sb(c, f"wo{l}", [P, KC, D])
            return b

        def ot_bank(k):
            return banks[:, k, :].rearrange("p (c n) -> p c n", c=KC)

        def output_sync(eng, l, b, wo):
            eng.dma_start(b["wo"][:, :, :], wo.rearrange("(c p) n -> p c n", p=P)).then_inc(sem(f"wo_in_{l}"), 16)

            def body(i, pos, seq, k, last):
                need(eng, f"o_turned_{l}", i - 1)
                src = o_d[l][seq * (WAVES // 2):(seq + 1) * (WAVES // 2), bass.ts(pos, P), :]
                eng.dma_start(b["o", k][:, :].rearrange("p (w d) -> p w d", d=2 * HD),
                              src.rearrange("w p d -> p w d")).then_inc(sem(f"o_in{k}_{l}"), 16)
            over_tiles(eng, body)
            if l == 1:
                for k in range(2):
                    eng.wait_ge(sem(f"out{k}"), 16 * NT // 2)

        def output_tensor(pe, l, b):
            credit(pe, l, "o_turned", "y_done")
            pe.wait_ge(sem(f"wo_in_{l}"), 16)

            def body(i, pos, seq, k, last):
                pe.wait_ge(sem(f"o_in{k}_{l}"), (i - k) * 8 + 16)
                need(pe, f"oT_ready_{l}", i - 1)
                for c in range(KC):
                    mm = nc.tensor.transpose(ot_bank(k)[:, c, :], b["o", k][:, c * P:(c + 1) * P], identf[:, :])
                mm.then_inc(sem(f"o_turned_{l}"), 1)
                need(pe, f"oT_ready_{l}", i + 1)
                need(pe, f"y_added_{l}", i - 1)
                for c in range(KC):
                    mm = nc.tensor.matmul(banks[:, 2 + k, :], b["oT", k][:, c, :], b["wo"][:, c, :],
                                          start=(c == 0), stop=(c == KC - 1))
                mm.then_inc(sem(f"y_done_{l}"), 1)
            over_tiles(pe, body)

        def output_scalar(act, l, b):
            credit(act, l, "oT_ready")

            def body(i, pos, seq, k, last):
                need(act, f"o_turned_{l}", i + 1)
                need(act, f"y_done_{l}", i - 1)
                nc.scalar.activation(b["oT", k][:, :, :], ot_bank(k), ACT.Copy).then_inc(sem(f"oT_ready_{l}"), 1)
                if l == 1:
                    need(act, "y_added_1", i + 1)
                    act.dma_start(out[bass.ts(i, P), :], b["res", k][:, :]).then_inc(sem(f"out{k}"), 16)
            over_tiles(act, body)

        def output_vector(v, l, b):
            credit(v, l, "y_added")

            def body(i, pos, seq, k, last):
                need(v, f"y_done_{l}", i + 1)
                if l == 1:
                    v.wait_ge(sem(f"out{k}"), (i - k) * 8)
                dst = b["res", k][:, :] if l else token_tile(i)
                nc.vector.tensor_tensor(dst, banks[:, 2 + k, :], token_tile(i), ALU.add)
                v.drain().then_inc(sem(f"y_added_{l}"), 1)
            over_tiles(v, body)

        def ffn_buffers(c):
            b = {}
            b["w"] = sb(c, "w_gu", [P, 2, KC, M])
            b["wd"] = sb(c, "w_down", [P, MC, D])
            b["h"] = sb(c, "h", [P, MC, TW])
            for k in range(2):
                b["x", k] = sb(c, f"ffn_x{k}", [P, KC, TW])
                b["sil", k] = sb(c, f"sil{k}", [P, TW])
                b["q", k] = sb(c, f"ffn_q{k}", [P, D], I32)
                b["am", k] = sb(c, f"ffn_am{k}", [P, D])
            for n in ("sign", "mag", "acc"):
                b[n] = sb(c, f"ffn_{n}", [P, D])
            return b

        def ffn_sync(eng, b):
            for m in range(2):
                for c in range(KC):
                    eng.dma_start(b["w"][:, m, c, :], w_d[m, c]).then_inc(sem("w_in"), 16)
            for k in range(2):
                eng.dma_start(b["x", k][:, :, :], xT_d[:, :, k * TW:(k + 1) * TW]).then_inc(sem(f"ffx_in{k}"), 16)
            with eng.Fori(0, MC // 2) as t:
                for k in range(2):
                    c = t * 2 + k
                    need(eng, "wd_ready_f", c - 1)
                    eng.dma_start(b["q", k][:, :], down_q[bass.ts(c, P), :]).then_inc(sem(f"wdq_in{k}"), 16)
                    for h in range(2):
                        eng.dma_start(b["am", k][64 * h:64 * h + 64, :],
                                      down_am[bass.ds(c * 2 + h, 1), :].to_broadcast([64, D])).then_inc(sem(f"wdq_in{k}"), 16)
            for k in range(2):
                need(eng, "gu_done_f", (k + 1) * MC)
                eng.dma_start(b["x", k][:, :, :], xT_d[:, :, (k + 2) * TW:(k + 3) * TW]).then_inc(sem(f"ffx_in{k}"), 16)

        def ffn_tensor(pe, b):
            credit(pe, "f", "gu_done", "down_done")
            pe.wait_ge(sem("w_in"), 16 * 2 * KC)
            with pe.Fori(0, TB // 2) as t:
                for k in range(2):
                    tb = t * 2 + k
                    pe.wait_ge(sem(f"ffx_in{k}"), t * 16 + 16)
                    for m in range(MC):
                        need(pe, "h_ready_f", tb * MC + (m - 1))
                        for u in range(2):
                            for c in range(KC):
                                mm = nc.tensor.matmul(banks[:, 2 * u + m % 2, :], b["w"][:, u, c, m * P:(m + 1) * P],
                                                      b["x", k][:, c, :], start=(c == 0), stop=(c == KC - 1))
                        mm.then_inc(sem("gu_done_f"), 1)
                    need(pe, "wd_ready_f", MC)
                    need(pe, "h_ready_f", (tb + 1) * MC)
                    for a in range(TW // P):
                        need(pe, "down_added_f", tb * (TW // P) + (a - 3))
                        for m in range(MC):
                            mm = nc.tensor.matmul(banks[:, 4 + a, :], b["h"][:, m, a * P:(a + 1) * P], b["wd"][:, m, :],
                                                  start=(m == 0), stop=(m == MC - 1))
                        mm.then_inc(sem("down_done_f"), 1)

        def ffn_scalar(act, b):
            credit(act, "f", "sil_ready")
            with act.Fori(0, TB) as tb:
                for m in range(MC):
                    need(act, "gu_done_f", tb * MC + (m + 1))
                    need(act, "h_ready_f", tb * MC + (m - 1))
                    nc.scalar.activation(b["sil", m % 2][:, :], banks[:, m % 2, :], ACT.Silu).then_inc(sem("sil_ready_f"), 1)

        def ffn_vector(v, b):
            dve = nc.vector
            credit(v, "f", "h_ready", "down_added", "wd_ready")

            def down_weights(c, k, t):
                v.wait_ge(sem(f"wdq_in{k}"), t * 48 + 48)
                dequantise(v, dve, b["q", k][:, :], b["am", k][:, :], b["wd"][:, c, :],
                           b["sign"][:, :], b["mag"][:, :], b["acc"][:, :])
                v.sem_inc(sem("wd_ready_f"), 1)

            def block(tb, first):
                for m in range(MC):
                    need(v, "sil_ready_f", tb * MC + (m + 1))
                    need(v, "down_done_f", tb * (TW // P))
                    dve.tensor_tensor(b["h"][:, m, :], banks[:, 2 + m % 2, :], b["sil", m % 2][:, :],
                                      ALU.mult).then_inc(sem("h_ready_f"), 1)
                    if first:
                        down_weights(m, m % 2, m // 2)
                for a in range(TW // P):
                    i = tb * (TW // P) + a
                    need(v, "down_done_f", i + 1)
                    dve.tensor_tensor(token_tile(i), banks[:, 4 + a, :], token_tile(i), ALU.add).then_inc(
                        sem("down_added_f"), 1)
            block(0, True)
            with v.Fori(1, TB) as tb:
                block(tb, False)

        layers = [(wqkv0, wo0), (wqkv1, wo1)]
        dq_ctx = ExitStack()
        dq = {}
        for k in range(2):
            dq["q", k] = sb(dq_ctx, f"dq_q{k}", [P, DQ], I32)
            dq["am", k] = sb(dq_ctx, f"dq_am{k}", [P, DQ])
            dq["res", k] = sb(dq_ctx, f"dq_res{k}", [P, DQ])
        for n in ("sign", "mag", "acc"):
            dq[n] = sb(dq_ctx, f"dq_{n}", [P, DQ])
        dq["token"] = sb(dq_ctx, "dq_token", [P, 1])
        bufs = {}
        for l in (0, 1):
            for name, make in (("project", project_buffers), ("attend", attend_buffers)):
                with ExitStack() as c:
                    bufs[name, l] = make(c, l)
            if l == 1:
                with ExitStack() as c:
                    bufs["ffn"] = ffn_buffers(c)
            with ExitStack() as c:
                bufs["output", l] = output_buffers(c, l)
            if l == 0:
                dq_ctx.close()

        block = ctx.enter_context(nc.Block())

        @block.sync
        def _(sp):
            sp.sem_inc(sem("started"), 1)
            for l, (wqkv, wo) in enumerate(layers):
                project_sync(sp, l, bufs["project", l], wqkv)
                barrier(sp, 4 * l + 1)
                attend_sync(sp, l, bufs["attend", l])
                barrier(sp, 4 * l + 2)
                if l == 1:
                    ffn_sync(sp, bufs["ffn"])
                barrier(sp, 4 * l + 3)
                output_sync(sp, l, bufs["output", l], wo)
                barrier(sp, 4 * l + 4)

        @block.tensor
        def _(pe):
            for l in (0, 1):
                project_tensor(pe, l, bufs["project", l])
                barrier(pe, 4 * l + 1)
                attend_tensor(pe, l, bufs["attend", l])
                barrier(pe, 4 * l + 2)
                if l == 1:
                    ffn_tensor(pe, bufs["ffn"])
                barrier(pe, 4 * l + 3)
                output_tensor(pe, l, bufs["output", l])
                barrier(pe, 4 * l + 4)

        @block.scalar
        def _(act):
            for l in (0, 1):
                project_scalar(act, l, bufs["project", l])
                barrier(act, 4 * l + 1)
                attend_scalar(act, l, bufs["attend", l])
                barrier(act, 4 * l + 2)
                if l == 1:
                    ffn_scalar(act, bufs["ffn"])
                barrier(act, 4 * l + 3)
                output_scalar(act, l, bufs["output", l])
                barrier(act, 4 * l + 4)

        @block.vector
        def _(v):
            for l in (0, 1):
                project_vector(v, l, bufs["project", l])
                barrier(v, 4 * l + 1)
                attend_vector(v, l, bufs["attend", l])
                barrier(v, 4 * l + 2)
                if l == 1:
                    ffn_vector(v, bufs["ffn"])
                barrier(v, 4 * l + 3)
                output_vector(v, l, bufs["output", l])
                barrier(v, 4 * l + 4)

        @block.gpsimd
        def _(pool):
            dequantise_gate_up(pool, dq)
            for n in range(POOL_JOINS, 6):
                barrier(pool, n)
            attend_gpsimd(pool, bufs["attend", 1])
            for n in range(6, 9):
                barrier(pool, n)


NF4 = [-1.0, -0.6961928009986877, -0.5250730514526367, -0.39491748809814453, -0.28444138169288635,
       -0.18477343022823334, -0.09105003625154495, 0.0, 0.07958029955625534, 0.16093020141124725,
       0.24611230194568634, 0.33791524171829224, 0.44070982933044434, 0.5626170039176941,
       0.7229568362236023, 1.0]


def shape_constants():
    import numpy as np
    from math import erf, exp, pi
    inv = (np.float32(1.0) / np.float32(10000.0) ** (np.arange(0, HD, 2, dtype=np.float32) / np.float32(HD))).astype(np.float32)
    angle = np.arange(SEQ, dtype=np.float32)[:, None] * inv[None, :]
    cos, sin = (np.float32(0.5) * f(angle).astype(np.float32) for f in (np.cos, np.sin))

    def normal_quantile(q):
        lo, hi = -10.0, 10.0
        for _ in range(60):
            mid = (lo + hi) / 2
            if 0.5 + 0.5 * erf(mid / 2 ** 0.5) < q:
                lo = mid
            else:
                hi = mid
        return lo

    quantile, kappa = np.zeros((P, NB), np.float32), np.zeros((P, NB), np.float32)
    for j in range(1, NB):
        for p in range(P):
            length = j * P + p + 1
            z = -normal_quantile((TOP - 4.0) / length)
            quantile[p, j] = z / (j * P) ** 0.5
            kappa[p, j] = (2 * pi) ** 0.5 * exp(z * z / 2) / length / (j * P) ** 0.5
    code = np.array(NF4)
    above, below = code[8:], -code[7::-1]
    at = np.vander(np.arange(8) - 3.5, 8)
    poly = [[float(np.float32(c)) for c in np.linalg.solve(at, y)] for y in ((above + below) / 2, (above - below) / 2)]
    return {
        "rope_cos": cos, "rope_sin": sin, "ident": np.eye(P, dtype=np.float32),
        "causal": np.where(np.arange(P)[:, None] < np.arange(P)[None, :], np.float32(NEG), np.float32(0)),
        "quantile": quantile, "kappa": kappa,
    }, poly


def lay_out(a):
    import numpy as np
    c = np.ascontiguousarray
    return {
        "x": c(a["L0_attn_x"].reshape(T, D)),
        "wqkv0": c(a["L0_attn_w_qkv"]), "wo0": c(a["L0_attn_w_o"]),
        "wup": c(a["L0_ffn_W_up"].T),
        "gate_lora": c(np.concatenate([a["L0_ffn_gate_w"], a["L0_ffn_lora_A"].reshape(NE * NR, D)]).T),
        "expert_bias": c(a["L0_ffn_expert_bias"].reshape(1, NE)),
        "lora_b": c(a["L0_ffn_lora_B"].transpose(0, 2, 1).reshape(NE * NR, D)),
        "wqkv1": c(np.concatenate([a["L1_attn_Wq"], a["L1_attn_Wk"], a["L1_attn_Wv"]]).T),
        "wo1": c(a["L1_attn_Wo"].T),
        "gate_q": c(a["L1_ffn_gate_q"].T), "gate_am": c(a["L1_ffn_gate_absmax"].reshape(M, D // 64).T),
        "up_q": c(a["L1_ffn_up_q"].T), "up_am": c(a["L1_ffn_up_absmax"].reshape(M, D // 64).T),
        "down_q": c(a["L1_ffn_down_q"].T), "down_am": c(a["L1_ffn_down_absmax"].reshape(D, M // 64).T),
    }


def kernel(**inputs):
    import numpy as np
    import concourse.bacc as bacc
    from concourse.bass_utils import run_bass_kernel_spmd

    constants, poly = shape_constants()
    arrays = {**lay_out({k: np.asarray(v) for k, v in inputs.items()}), **constants}
    nc = bacc.Bacc("TRN2", target_bir_lowering=False, num_devices=1)
    args = {n: nc.dram_tensor(f"in_{n}", a.shape, mybir.dt.from_np(a.dtype), kind="ExternalInput").ap()
            for n, a in arrays.items()}
    out = nc.dram_tensor("out_y", (T, D), F32, kind="ExternalOutput").ap()
    kernel_program(nc, poly, out=out, **args)
    r = run_bass_kernel_spmd(nc, [{f"in_{n}": a for n, a in arrays.items()}], core_ids=[0])
    return r.results[0]["out_y"].reshape(2, SEQ, D)
```

```python
from contextlib import ExitStack

import concourse.bass as bass
from concourse import mybir

F32 = mybir.dt.float32
BF16 = mybir.dt.bfloat16
I32 = mybir.dt.int32
ALU = mybir.AluOpType
ACT = mybir.ActivationFunctionType
AX = mybir.AxisListType

P = 128
T = 2048
D = 512
KC = D // P
NT = T // P
SEQ = 1024
NB = SEQ // P
H, KV, HD = 32, 8, 16
HALF = HD // 2
QK = (H + KV) * HD
QKV = QK + KV * HD
RB = QK // P
NE, NR = 4, 8
M = 1792
MC = M // P
TOP = 128
WINDOW = 8
WAVES = 32
NEG = -1.0e30
TAKEN = -3.0e38
NTILE = 2 * NB
SCOL = [P * j * (j + 1) // 2 for j in range(NB + 1)]
TB = 4
TW = T // TB
DQ = M // 4
CREDIT = 64
ONE_DMA = 16
DOWN_EARLY = 5
POOL_JOINS = 4


def kernel_program(nc, poly, x, wqkv0, wo0, wup, gate_lora, expert_bias, lora_b, wqkv1, wo1,
                   gate_q, gate_am, up_q, up_am, down_q, down_am,
                   rope_cos, rope_sin, ident, causal, quantile, kappa, out):
    qkT = [nc.dram_tensor(f"qkT_{l}", [3, 2, QK, SEQ], BF16, kind="Internal").ap() for l in (0, 1)]
    v_d = [nc.dram_tensor(f"v_rows_{l}", [2, SEQ, KV * HD], F32, kind="Internal").ap() for l in (0, 1)]
    o_d = [nc.dram_tensor(f"attended_{l}", [WAVES, SEQ, 2 * HD], F32, kind="Internal").ap() for l in (0, 1)]
    xT_d = nc.dram_tensor("xT_rows", [P, KC, T], F32, kind="Internal").ap()
    w_d = nc.dram_tensor("gate_up_weights", [2, KC, P, M], F32, kind="Internal").ap()
    wd_d = nc.dram_tensor("down_weights", [MC, P, D], F32, kind="Internal").ap()

    ctx = ExitStack()
    with ctx:
        sems = {}

        def sem(name):
            if name not in sems:
                sems[name] = ctx.enter_context(nc.semaphore(name))
            return sems[name]

        def sb(c, name, shape, dt=F32):
            return c.enter_context(nc.sbuf_tensor(name, shape, dt))

        resid = sb(ctx, "resid", [P, NT, D])
        identf = sb(ctx, "identf", [P, P])
        identb = sb(ctx, "identb", [P, P], BF16)
        fold = sb(ctx, "fold", [P, HD])
        causalf = sb(ctx, "causalf", [P, P])
        causalb = sb(ctx, "causalb", [P, P], BF16)
        banks = ctx.enter_context(nc.psum_tensor("banks", [P, 8, 512], F32))

        def stand_alone(eng):
            eng.wait_ge(sem("started"), 1)

        def credit_dma(eng, *names):
            for n in names:
                eng.sem_inc(sem(n), ONE_DMA)

        def credit(eng, l, *names):
            for n in names:
                eng.sem_inc(sem(f"{n}_{l}"), CREDIT)

        def barrier(eng, n):
            own = "pool_phase_ended" if eng is nc.gpsimd else "phase_ended"
            eng.drain().then_inc(sem(own), 1)
            eng.wait_ge(sem("phase_ended"), 4 * n)
            if n >= POOL_JOINS:
                eng.wait_ge(sem("pool_phase_ended"), n - POOL_JOINS + 1)

        def token_tile(i):
            return resid[:, bass.ds(i, 1), :].rearrange("p a n -> p (a n)")

        def over_tiles(eng, body):
            for seq in range(2):
                with eng.Fori(0, NB // 2 - seq) as t:
                    for k in range(2):
                        body(t * 2 + (k + seq * NB), t * 2 + k, seq, k, False)
            for k in range(2):
                body(NT - 2 + k, NB - 2 + k, 1, k, k == 1)

        def over_waves(eng, wave):
            with eng.Fori(0, WAVES // 2 - 1) as t:
                for k in range(2):
                    wave(t * 2 + k, k, 2)
            wave(WAVES - 2, 0, 1)
            wave(WAVES - 1, 1, 0)

        def project_buffers(c, l):
            b = {}
            for k in range(2):
                if l == 0:
                    b["xin", k] = sb(c, f"xin{k}", [P, D])
                b["xn", k] = sb(c, f"xn{l}{k}", [P, D])
                b["xT", k] = sb(c, f"xT{l}{k}", [P, KC, P])
                b["st", k] = sb(c, f"st{l}{k}", [P, 6])
                b["mv", k] = sb(c, f"mv{l}{k}", [P, 2])
                b["sd", k] = sb(c, f"sd{l}{k}", [P, 1])
                b["rs", k] = sb(c, f"rs{l}{k}", [P, 1])
                b["r", k] = sb(c, f"r{l}{k}", [P, QK])
                b["parts", k] = sb(c, f"parts{l}{k}", [P, 3, RB, P], BF16)
                b["v", k] = sb(c, f"v{l}{k}", [P, KV * HD])
                b["zm", k] = sb(c, f"zm{l}{k}", [P, NE * NR])
                b["zT", k] = sb(c, f"zT{l}{k}", [NE * NR, P])
            for n in range(4):
                b["t", n] = sb(c, f"rope_t{l}{n}", [P, H + KV, HALF])
            b["d1"] = sb(c, f"d1{l}", [P, RB, P])
            b["wqkv"] = sb(c, f"wqkv{l}", [P, KC, QKV])
            b["cos"] = sb(c, f"cos{l}", [P, NB, HALF])
            b["sin"] = sb(c, f"sin{l}", [P, NB, HALF])
            b["eps"] = sb(c, f"eps{l}", [P, 1])
            if l == 0:
                b["wup"] = sb(c, "wup", [P, KC, D])
                b["gl"] = sb(c, "gl", [P, KC, NE + NE * NR])
                b["lb"] = sb(c, "lb", [NE * NR, D])
                b["bias"] = sb(c, "bias", [P, NE])
                b["rank"] = sb(c, "rank", [P, NE])
                for n in ("lg", "eq", "key", "oh"):
                    b[n] = sb(c, n, [P, NE])
                for n in ("mx", "mk"):
                    b[n] = sb(c, n, [P, 1])
            return b

        QKV_PS = banks[:, 0:2, :].rearrange("p a n -> p (a n)")
        UP_PS = banks[:, 2, :]
        TX_PS = banks[:, 3, :].rearrange("p (c n) -> p c n", c=KC)
        TR_PS = banks[:, 4:6, :].rearrange("p a n -> p (a n)")[:, 0:QK].rearrange("p (c n) -> p c n", c=RB)
        GL_PS = banks[:, 6, 0:NE + NE * NR]
        ZT_PS = banks[0:NE * NR, 7, 0:P]
        N_WEIGHTS = [9, 3]
        N_STORES = [4, 5]

        def slot_stores(l, i, k):
            return (i - k) * 8 * N_STORES[l]

        def project_sync(eng, l, b, wqkv):
            def s(n):
                return sem(f"{n}_{l}")
            credit_dma(eng, f"stored0_{l}", f"stored1_{l}")
            loads = [(b["wqkv"][:, :, :], wqkv.rearrange("(c p) n -> p c n", p=P)),
                     (b["cos"][:, :, :], rope_cos.rearrange("(c p) n -> p c n", p=P)),
                     (b["sin"][:, :, :], rope_sin.rearrange("(c p) n -> p c n", p=P))]
            if l == 0:
                for k in range(2):
                    eng.dma_start(b["xin", k][:, :], x[k * P:(k + 1) * P, :]).then_inc(s(f"x_in{k}"), 16)
                loads += [(identf[:, :], ident), (causalf[:, :], causal),
                          (b["wup"][:, :, :], wup.rearrange("(c p) n -> p c n", p=P)),
                          (b["gl"][:, :, :], gate_lora.rearrange("(c p) n -> p c n", p=P)),
                          (b["lb"][:, :], lora_b),
                          (b["bias"][:, :], expert_bias.to_broadcast([P, NE]))]
            for dst, src in loads:
                eng.dma_start(dst, src).then_inc(s("weights_in"), 16)

            def body(i, pos, seq, k, last):
                eng.wait_ge(sem(f"parts_ready_{l}"), CREDIT + i + 1)
                stand_alone(eng)
                for part in range(3):
                    dst = qkT[l][part, seq].rearrange("(c p) t -> p c t", p=P)
                    eng.dma_start(dst[:, :, bass.ts(pos, P)], b["parts", k][:, part]).then_inc(s(f"stored{k}"), 16)
                if l == 1:
                    eng.wait_ge(sem(f"xT_ready_{l}"), CREDIT + i + 1)
                    stand_alone(eng)
                eng.wait_ge(sem(f"qkv_free_{l}"), CREDIT + i + 1)
                stand_alone(eng)
                eng.dma_start(v_d[l][seq][bass.ts(pos, P), :], b["v", k][:, :]).then_inc(s(f"stored{k}"), 16)
                if l == 1:
                    eng.dma_start(xT_d[:, :, bass.ts(i, P)], b["xT", k][:, :, :]).then_inc(s(f"stored{k}"), 16)
                elif not (isinstance(i, int)):
                    eng.wait_ge(sem("x_used_0"), CREDIT + i + 1)
                    stand_alone(eng)
                    eng.dma_start(b["xin", k][:, :], x[bass.ts(i + 2, P), :]).then_inc(s(f"x_in{k}"), 16)
            over_tiles(eng, body)
            for k in range(2):
                eng.wait_ge(sem(f"stored{k}_{l}"), ONE_DMA + slot_stores(l, NT + k, k))

        def project_tensor(pe, l, b):
            def transpose_x(i, k):
                pe.wait_ge(sem(f"xn_ready_{l}"), CREDIT + i + 1)
                for c in range(KC):
                    mm = nc.tensor.transpose(TX_PS[:, c, :], b["xn", k][:, c * P:(c + 1) * P], identf[:, :])
                mm.then_inc(sem(f"x_transposed_{l}"), 1)

            credit(pe, l, "x_transposed", "qkv_done", "gl_done", "r_transposed", "z_transposed", "up_done")
            pe.wait_ge(sem(f"weights_in_{l}"), 16 * N_WEIGHTS[l])
            transpose_x(0, 0)

            def body(i, pos, seq, k, last):
                pe.wait_ge(sem(f"xT_ready_{l}"), CREDIT + i + 1)
                pe.wait_ge(sem(f"qkv_free_{l}"), CREDIT + i)
                for lo, hi in ((0, 512), (512, QKV)):
                    for c in range(KC):
                        mm = nc.tensor.matmul(QKV_PS[:, lo:hi], b["xT", k][:, c, :], b["wqkv"][:, c, lo:hi],
                                              start=(c == 0), stop=(c == KC - 1))
                mm.then_inc(sem(f"qkv_done_{l}"), 1)
                if l == 0:
                    pe.wait_ge(sem("x_used_0"), CREDIT + i)
                    for c in range(KC):
                        nc.tensor.matmul(UP_PS, b["xT", k][:, c, :], b["wup"][:, c, :], start=(c == 0), stop=False)
                    pe.wait_ge(sem("zm_ready_0"), CREDIT + i)
                    for c in range(KC):
                        mm = nc.tensor.matmul(GL_PS, b["xT", k][:, c, :], b["gl"][:, c, :],
                                              start=(c == 0), stop=(c == KC - 1))
                    mm.then_inc(sem("gl_done_0"), 1)
                if not last:
                    transpose_x(i + 1, 1 - k)
                pe.wait_ge(sem(f"r_ready_{l}"), CREDIT + i + 1)
                pe.wait_ge(sem(f"tr_free_{l}"), CREDIT + i)
                for c in range(RB):
                    mm = nc.tensor.transpose(TR_PS[:, c, :], b["r", k][:, c * P:(c + 1) * P], identf[:, :])
                mm.then_inc(sem(f"r_transposed_{l}"), 1)
                if l == 0:
                    pe.wait_ge(sem("zm_ready_0"), CREDIT + i + 1)
                    nc.tensor.transpose(ZT_PS, b["zm", k][:, :], identf[:, :]).then_inc(sem("z_transposed_0"), 1)
                    pe.wait_ge(sem("zT_ready_0"), CREDIT + i + 1)
                    nc.tensor.matmul(UP_PS, b["zT", k][:, :], b["lb"][:, :], start=False,
                                     stop=True).then_inc(sem("up_done_0"), 1)
            over_tiles(pe, body)

        def project_scalar(act, l, b):
            def head(i, k):
                act.wait_ge(sem(f"var_ready_{l}"), CREDIT + i + 1)
                nc.scalar.activation(b["sd", k][:, :], b["mv", k][:, 1:2], ACT.Sqrt,
                                     bias=b["eps"][:, :]).then_inc(sem(f"sd_ready_{l}"), 1)

            def copy_x(i, k):
                act.wait_ge(sem(f"x_transposed_{l}"), CREDIT + i + 1)
                nc.scalar.activation(b["xT", k][:, :, :], TX_PS, ACT.Copy).then_inc(sem(f"xT_ready_{l}"), 1)

            credit(act, l, "sd_ready", "xT_ready", "part1_ready", "zT_ready")
            act.wait_ge(sem(f"consts_ready_{l}"), 1)
            head(0, 0)
            copy_x(0, 0)

            def body(i, pos, seq, k, last):
                if not last:
                    head(i + 1, 1 - k)
                    act.wait_ge(sem(f"qkv_done_{l}" if l else "gl_done_0"), CREDIT + i)
                    if l:
                        act.wait_ge(sem(f"stored{1 - k}_1"), ONE_DMA + slot_stores(l, i + 1, 1 - k))
                    copy_x(i + 1, 1 - k)
                act.wait_ge(sem(f"r_transposed_{l}"), CREDIT + i + 1)
                act.wait_ge(sem(f"stored{k}_{l}"), ONE_DMA + slot_stores(l, i, k))
                nc.scalar.activation(b["parts", k][:, 0], TR_PS, ACT.Copy).then_inc(sem(f"part1_ready_{l}"), 1)
                if l == 0:
                    act.wait_ge(sem("z_transposed_0"), CREDIT + i + 1)
                    nc.scalar.activation(b["zT", k][:, :], ZT_PS, ACT.Copy).then_inc(sem("zT_ready_0"), 1)
            over_tiles(act, body)

        def project_vector(v, l, b):
            dve = nc.vector
            credit(v, l, "var_ready", "xn_ready", "qkv_free", "r_ready", "zm_ready", "tr_free",
                   "parts_ready", "x_used")
            dve.memset(b["eps"][:, :], 1e-5)
            if l == 0:
                for e in range(NE):
                    dve.memset(b["rank"][:, e:e + 1], float(NE - e))
            v.drain().then_inc(sem(f"consts_ready_{l}"), 1)
            v.wait_ge(sem(f"weights_in_{l}"), 16 * N_WEIGHTS[l])
            if l == 0:
                dve.tensor_copy(identb[:, :], identf[:, :])
                dve.tensor_copy(causalb[:, :], causalf[:, :])
                dve.tensor_copy(fold[:, :], identf[:, 0:HD])
                for g in range(1, 4):
                    v.drain()
                    dve.tensor_tensor(fold[:, :], fold[:, :], identf[:, 32 * g:32 * g + HD], ALU.add)

            def norm(i, k):
                if l == 0:
                    src = b["xin", k][:, :]
                    v.wait_ge(sem(f"x_in{k}_0"), (i - k) * 8 + 16)
                else:
                    src = token_tile(i)
                dve.bn_stats(b["st", k][:, :], src)
                v.drain()
                dve.bn_aggr(b["mv", k][:, :], b["st", k][:, :])
                v.drain().then_inc(sem(f"var_ready_{l}"), 1)
                v.wait_ge(sem(f"sd_ready_{l}"), CREDIT + i + 1)
                dve.reciprocal(b["rs", k][:, :], b["sd", k][:, :])
                v.drain()
                v.wait_ge(sem(f"x_transposed_{l}"), CREDIT + i - 1)
                dve.tensor_scalar(b["xn", k][:, :], src, b["mv", k][:, 0:1], b["rs", k][:, :],
                                  ALU.subtract, ALU.mult).then_inc(sem(f"xn_ready_{l}"), 1)

            norm(0, 0)

            def body(i, pos, seq, k, last):
                if not last:
                    norm(i + 1, 1 - k)
                v.wait_ge(sem(f"qkv_done_{l}"), CREDIT + i + 1)
                if l == 0:
                    hv = QKV_PS[:, 0:QK].rearrange("p (h i two) -> p h two i", h=H + KV, two=2)
                else:
                    hv = QKV_PS[:, 0:QK].rearrange("p (h two i) -> p h two i", h=H + KV, two=2)
                x1, x2 = hv[:, :, 0, :], hv[:, :, 1, :]
                cos = b["cos"][:, bass.ds(pos, 1), :].to_broadcast([P, H + KV, HALF])
                sin = b["sin"][:, bass.ds(pos, 1), :].to_broadcast([P, H + KV, HALF])
                for n, (src, tab) in enumerate(((x1, cos), (x2, sin), (x1, sin), (x2, cos))):
                    dve.tensor_tensor(b["t", n][:, :, :], src, tab, ALU.mult)
                v.wait_ge(sem(f"stored{k}_{l}"), ONE_DMA + slot_stores(l, i, k))
                dve.tensor_copy(b["v", k][:, :], QKV_PS[:, QK:QKV])
                v.drain().then_inc(sem(f"qkv_free_{l}"), 1)
                v.wait_ge(sem(f"r_transposed_{l}"), CREDIT + i - 1)
                rv = b["r", k][:, :].rearrange("p (h two i) -> p h two i", h=H + KV, two=2)
                dve.tensor_tensor(rv[:, :, 0, :], b["t", 0][:, :, :], b["t", 1][:, :, :], ALU.subtract)
                dve.tensor_tensor(rv[:, :, 1, :], b["t", 2][:, :, :], b["t", 3][:, :, :], ALU.add)
                v.drain().then_inc(sem(f"r_ready_{l}"), 1)
                if l == 0:
                    v.wait_ge(sem("gl_done_0"), CREDIT + i + 1)
                    dve.tensor_tensor(b["lg"][:, :], GL_PS[:, 0:NE], b["bias"][:, :], ALU.add)
                    v.drain()
                    dve.tensor_reduce(b["mx"][:, :], b["lg"][:, :], AX.X, ALU.max)
                    v.drain()
                    dve.tensor_scalar(b["eq"][:, :], b["lg"][:, :], b["mx"][:, :], None, ALU.is_ge)
                    v.drain()
                    dve.tensor_tensor(b["key"][:, :], b["eq"][:, :], b["rank"][:, :], ALU.mult)
                    v.drain()
                    dve.tensor_reduce(b["mk"][:, :], b["key"][:, :], AX.X, ALU.max)
                    v.drain()
                    dve.tensor_scalar(b["oh"][:, :], b["key"][:, :], b["mk"][:, :], None, ALU.is_equal)
                    v.drain()
                    v.wait_ge(sem("z_transposed_0"), CREDIT + i - 1)
                    dve.tensor_tensor(b["zm", k][:, :].rearrange("p (e r) -> p e r", e=NE),
                                      GL_PS[:, NE:].rearrange("p (e r) -> p e r", e=NE),
                                      b["oh"][:, :].rearrange("p (e a) -> p e a", a=1).to_broadcast([P, NE, NR]),
                                      ALU.mult).then_inc(sem("zm_ready_0"), 1)
                v.wait_ge(sem(f"part1_ready_{l}"), CREDIT + i + 1)
                dve.tensor_tensor(b["d1"][:, :, :], TR_PS, b["parts", k][:, 0], ALU.subtract)
                v.drain().then_inc(sem(f"tr_free_{l}"), 1)
                dve.tensor_copy(b["parts", k][:, 1], b["d1"][:, :, :])
                v.drain()
                dve.tensor_tensor(b["parts", k][:, 2], b["d1"][:, :, :], b["parts", k][:, 1], ALU.subtract)
                v.drain().then_inc(sem(f"parts_ready_{l}"), 1)
                if l == 0:
                    v.wait_ge(sem("up_done_0"), CREDIT + i + 1)
                    dve.tensor_tensor(token_tile(i), UP_PS, b["xin", k][:, :], ALU.add)
                    v.drain().then_inc(sem("x_used_0"), 1)
            over_tiles(v, body)

        def dequantise(eng, e, q, am, res, sign, mag, acc):
            def op(*a):
                e.tensor_scalar(*a)
                eng.drain()

            def op2(*a):
                e.tensor_tensor(*a)
                eng.drain()
            op(mag, q, 1.0, -7.5, ALU.mult, ALU.add)
            op(sign, mag, 2.0, 1.0, ALU.mult, ALU.mult)
            op(sign, sign, 1.0, -1.0, ALU.min, ALU.max)
            op2(mag, mag, sign, ALU.mult)
            op(mag, mag, 1.0, -4.0, ALU.mult, ALU.add)
            for y, co in ((acc, poly[0]), (res, poly[1])):
                op(y, mag, co[0], co[1], ALU.mult, ALU.add)
                for c in co[2:]:
                    op2(y, y, mag, ALU.mult)
                    op(y, y, 1.0, c, ALU.mult, ALU.add)
            op2(acc, acc, sign, ALU.mult)
            op2(res, res, acc, ALU.add)
            op2(res, res, am, ALU.mult)

        def dequantise_gate_up(pool, b):
            nc.gpsimd.memset(b["token"][:, :], 0.0)
            pool.drain()
            for m, (q_d, am_d) in enumerate(((gate_q, gate_am), (up_q, up_am))):
                with pool.Fori(0, KC) as c:
                    for u in range(4):
                        k, n = u % 2, (c + m * KC) * 2 + u // 2
                        cols = slice(u * DQ, (u + 1) * DQ)
                        pool.dma_start(b["q", k][:, :], q_d[bass.ts(c, P), cols]).then_inc(sem(f"dq_moved{k}"), 16)
                        for h in range(2):
                            pool.dma_start(b["am", k][64 * h:64 * h + 64, :],
                                           am_d[bass.ds(c * 2 + h, 1), cols].to_broadcast([64, DQ])
                                           ).then_inc(sem(f"dq_moved{k}"), 16)
                        pool.wait_ge(sem(f"dq_moved{k}"), n * 64 + 48)
                        nc.gpsimd.tensor_tensor(b["token"][:, :], b["token"][:, :], b["token"][:, :], ALU.mult)
                        dequantise(pool, nc.gpsimd, b["q", k][:, :], b["am", k][:, :], b["res", k][:, :],
                                   b["sign"][:, :], b["mag"][:, :], b["acc"][:, :])
                        pool.dma_start(w_d[m][bass.ds(c, 1), :, cols].rearrange("a p n -> (a p) n"),
                                       b["res", k][:, :]).then_inc(sem(f"dq_moved{k}"), 16)
            for k in range(2):
                pool.wait_ge(sem(f"dq_moved{k}"), 64 * 4 * KC)

        def attend_buffers(c, l):
            b = {}
            for k in range(2):
                b["K", k] = sb(c, f"K{l}{k}", [P, SEQ], BF16)
                b["Q", k] = sb(c, f"Q{l}{k}", [P, 2, SEQ], BF16)
                b["V", k] = sb(c, f"V{l}{k}", [P, NB, 32])
                b["O", k] = sb(c, f"O{l}{k}", [P, NB, 2 * HD])
                b["OT", k] = sb(c, f"OT{l}{k}", [P, 4, P])
                b["sum", k] = sb(c, f"sum{l}{k}", [P, 2, NB])
                b["rsum", k] = sb(c, f"rsum{l}{k}", [P, 2, NB])
                b["PT", k] = sb(c, f"PT{l}{k}", [P, NB, P])
                b["nmax", k] = sb(c, f"nmax{l}{k}", [P, 2, NB])
                b["P", k] = sb(c, f"P{l}{k}", [P, SEQ])
            b["zeroV"] = sb(c, f"zeroV{l}", [P, 32])
            if l == 1:
                for k in range(2):
                    b["S", k] = sb(c, f"S{k}", [P, 2, SCOL[NB]])
                    for n in STATE:
                        b[n, k] = sb(c, f"{n}{k}", [P, 2, NB])
                    b["junk", k] = sb(c, f"junk{k}", [P, SEQ], BF16)
                for n in [f"{e}{n}" for e in "pv" for n in range(1, 9)] + ["theta", "half", "minus", "cols"]:
                    b[n] = sb(c, n, [P, 2, NB])
                for k in range(3):
                    b["Y", k] = sb(c, f"Y{k}", [P, SEQ])
                b["E"] = sb(c, "E", [P, SCOL[NB]])
                b["top8"] = sb(c, "top8", [P, 2, NB, 8])
                b["pick"] = sb(c, "pick", [P, 2, NB, 8])
                b["iota8"] = sb(c, "iota8", [P, 8])
                b["after"] = sb(c, "after", [P, 2, NB, 8])
                b["settled"] = sb(c, "settled", [P, 2, NB])
                b["open"] = sb(c, "open", [P, 32])
                b["openT"] = sb(c, "openT", [P, 32])
                b["row"] = sb(c, "row", [P, 1])
                b["any"] = sb(c, "any", [1, 1], I32)
                b["quant"] = sb(c, "quant", [P, NB])
                b["kappa"] = sb(c, "kappa", [P, NB])
            return b

        STATE = ("max", "ssq", "t", "nt", "cnt", "lo", "clo", "hi", "chi", "kap", "blo", "bhi")

        def width(j):
            return P * (j + 1)

        ACT_PASSES = 4 * 2 * (NB - 1) + NB - 1

        def s_ps(n):
            return banks[:, 2 * (n % 2):2 * (n % 2) + 2, :].rearrange("p a n -> p (a n)")

        def pt_ps(m):
            return banks[:, 4 + m % 2, :].rearrange("p (c q) -> p c q", c=4)

        OT_PS = banks[:, 6, :].rearrange("p (a q) -> p a q", a=4)
        OQ_PS = banks[:, 7, 0:4 * HD].rearrange("p (a d) -> p a d", a=4)
        HALVES = [1 if j < 4 else 2 for j in range(NB)]
        PT_AT = [sum((HALVES * 2)[:n]) for n in range(NTILE + 1)]
        PT_WAVE = PT_AT[NTILE]

        def attend_sync(eng, l, b):
            def s(n):
                return sem(f"{n}_{l}")
            credit_dma(eng, f"o_out0_{l}", f"o_out1_{l}")
            if l == 1:
                eng.dma_start(b["quant"][:, :], quantile).then_inc(sem("tables_in"), 16)
                eng.dma_start(b["kappa"][:, :], kappa).then_inc(sem("tables_in"), 16)
            with eng.Fori(0, 2) as q:
                with eng.Fori(0, KV) as g:
                    for k in range(2):
                        w = (q * KV + g) * 2 + k
                        eng.wait_ge(sem(f"s_done_{l}"), CREDIT + (w - 1) * NTILE)
                        stand_alone(eng)
                        for part in range(3):
                            rows = qkT[l][part][bass.ds(q, 1)].rearrange("a r t -> (a r) t")
                            kr = rows[bass.ds(g * HD + H * HD, HD), :]
                            qr = rows[bass.ds(g * 4 * HD + k * 2 * HD, 2 * HD), :].rearrange("(h d) t -> d h t", d=HD)
                            for rep in range(3 if part < 2 else 2):
                                at = (3 * part + rep) * HD
                                eng.dma_start(b["Q", k][at:at + HD, :, :], qr).then_inc(s(f"qk_in{k}"), 16)
                                at = (part + 3 * rep) * HD
                                eng.dma_start(b["K", k][at:at + HD, :], kr).then_inc(s(f"qk_in{k}"), 16)
                        eng.wait_ge(sem(f"value_done_{l}"), CREDIT + (w - 1) * NTILE)
                        stand_alone(eng)
                        vr = v_d[l][bass.ds(q, 1)].rearrange("a (c p) d -> (a p) c d", p=P)
                        eng.dma_start(b["V", k][:, :, 0:HD], vr[:, :, bass.ds(g * HD, HD)]).then_inc(s(f"v_in{k}"), 16)
            for k in range(2):
                eng.wait_ge(sem(f"o_out{k}_{l}"), ONE_DMA + 16 * WAVES // 2)

        def attend_tensor(pe, l, b):
            def scores(n, k, w):
                r, j = divmod(n, NB)
                if n == 0:
                    pe.wait_ge(sem(f"qk_in{k}_{l}"), (w - k + 2) * 128)
                ps = s_ps(n)
                pe.wait_ge(sem(("p_ready_0", "s_stored_1")[l]), CREDIT + w * NTILE + (n - 1))
                for lo in range(0, width(j), 512):
                    hi = min(lo + 512, width(j))
                    nc.tensor.matmul(ps[:, lo:hi], b["Q", k][:, r, j * P:(j + 1) * P], b["K", k][:, lo:hi],
                                     start=True, stop=(hi != width(j)))
                nc.tensor.matmul(ps[:, j * P:(j + 1) * P], identb[:, :], causalb[:, :],
                                 start=False, stop=True).then_inc(sem(f"s_done_{l}"), 1)

            def turn(n, k, w):
                pe.wait_ge(sem(f"p_ready_{l}"), CREDIT + w * NTILE + (n + 1))
                j = n % NB
                for h in range(HALVES[j]):
                    m = PT_AT[n] + h
                    pe.wait_ge(sem(f"pt_used{m % 2}_{l}"), CREDIT + w * (PT_WAVE // 2) + m // 2)
                    for c in range(min(4, j + 1 - 4 * h)):
                        at = (4 * h + c) * P
                        mm = nc.tensor.transpose(pt_ps(m)[:, c, :], b["P", n % 2][:, at:at + P], identf[:, :])
                    mm.then_inc(sem(f"turned_{l}"), 1)

            def values(n, k, w):
                j = n % NB
                if n == 0:
                    pe.wait_ge(sem(f"v_in{k}_{l}"), (w - k + 2) * 8)
                pe.wait_ge(sem(f"pt_used0_{l}"), CREDIT + w * (PT_WAVE // 2) + (PT_AT[n + 1] + 1) // 2)
                pe.wait_ge(sem(f"pt_used1_{l}"), CREDIT + w * (PT_WAVE // 2) + PT_AT[n + 1] // 2)
                if n % 4 == 0:
                    pe.wait_ge(sem(f"ot_copied_{l}"), CREDIT + w * 4 + n // 4)
                for g in range(j + 1, 4):
                    nc.tensor.matmul(OT_PS[32 * g:32 * g + 32, j % 4, :], b["zeroV"][:, :], b["PT", n % 2][:, 0, :],
                                     start=True, stop=True)
                for c in range(j + 1):
                    g = c % 4
                    mm = nc.tensor.matmul(OT_PS[32 * g:32 * g + 32, j % 4, :], b["V", k][:, c, :],
                                          b["PT", n % 2][:, c, :], start=(c < 4), stop=(c + 4 > j))
                mm.then_inc(sem(f"value_done_{l}"), 1)

            def rows(m, w):
                pe.wait_ge(sem(f"ot_copied_{l}"), CREDIT + w * 4 + (m + 1))
                pe.wait_ge(sem(f"oq_read_{l}"), CREDIT + w * 4 + m)
                for a in range(4):
                    mm = nc.tensor.matmul(OQ_PS[:, a, :], b["OT", m % 2][:, a, :], fold[:, :], start=True, stop=True)
                mm.then_inc(sem(f"rows_done_{l}"), 1)

            def wave(w, k, left):
                if l == 1 and left == 2:
                    for n in range(2):
                        scores(n, k, w + 2)
                for n in range(NTILE):
                    if l == 0 and n + 2 < NTILE:
                        scores(n + 2, k, w)
                    elif l == 0 and left:
                        scores(n + 2 - NTILE, 1 - k, w + 1)
                    turn(n, k, w)
                    if n > 0:
                        values(n - 1, k, w)
                    if n % 4 == 1 and n > 1:
                        rows(n // 4 - 1, w)
                    if l == 1 and left == 2 and 0 < n < NTILE - 1:
                        scores(n + 1, k, w + 2)
                values(NTILE - 1, k, w)
                rows(3, w)

            credit(pe, l, "s_done", "turned", "value_done", "rows_done")
            pe.wait_ge(sem(f"att_consts_{l}"), 1)
            if l == 0:
                for n in range(2):
                    scores(n, 0, 0)
            else:
                for w in range(2):
                    for n in range(NTILE):
                        scores(n, w, w)
            over_waves(pe, wave)

        def pt_copy(eng, copy, l, b, n, w, h):
            m = PT_AT[n] + h
            blocks = min(4, n % NB + 1 - 4 * h)
            eng.wait_ge(sem(f"turned_{l}"), CREDIT + w * PT_WAVE + (m + 1))
            eng.wait_ge(sem(f"value_done_{l}"), CREDIT + w * NTILE + (n - 1))
            copy(b["PT", n % 2][:, 4 * h:4 * h + blocks, :], pt_ps(m)[:, 0:blocks, :]).then_inc(
                sem(f"pt_used{m % 2}_{l}"), 1)

        def attend_scalar(act, l, b):
            def copy(dst, src):
                return nc.scalar.activation(dst, src, ACT.Copy)

            def ot_copy(m, w):
                act.wait_ge(sem(f"value_done_{l}"), CREDIT + w * NTILE + (4 * m + 4))
                act.wait_ge(sem(f"rows_done_{l}"), CREDIT + w * 4 + (m - 1))
                copy(b["OT", m % 2][:, :, :], OT_PS).then_inc(sem(f"ot_copied_{l}"), 1)

            def store(k, w):
                act.wait_ge(sem(f"o_ready_{l}"), CREDIT + w * 4 + 4)
                act.dma_start(o_d[l][bass.ds(w, 1)].rearrange("a (c p) d -> (a p) c d", p=P),
                              b["O", k][:, :, :]).then_inc(sem(f"o_out{k}_{l}"), 16)

            def exp0(n, k, w):
                r, j = divmod(n, NB)
                act.wait_ge(sem("max_ready_0"), CREDIT + w * NTILE + (n + 1))
                before = PT_AT[n - 1] if n >= 2 else PT_AT[n + NTILE - 1] - PT_WAVE
                act.wait_ge(sem("turned_0"), CREDIT + w * PT_WAVE + before)
                nc.scalar.activation(b["P", n % 2][:, 0:width(j)], s_ps(n)[:, 0:width(j)], ACT.Exp,
                                     bias=b["nmax", k][:, r, j:j + 1],
                                     accum_out=b["sum", k][:, r, j:j + 1]).then_inc(sem("p_ready_0"), 1)

            def wave0(w, k, left):
                for n in range(NTILE):
                    if n + 1 < NTILE:
                        exp0(n + 1, k, w)
                    elif left:
                        exp0(0, 1 - k, w + 1)
                    if HALVES[n % NB] == 2:
                        pt_copy(act, copy, l, b, n, w, 1)
                    if n % 4 == 0 and n > 0:
                        ot_copy(n // 4 - 1, w)
                ot_copy(3, w)
                store(k, w)

            NJ = NB - 1
            PASS = 2 * NJ

            def square(n, k, w):
                r, j = divmod(n, NB)
                if j:
                    act.wait_ge(sem("s_stored_1"), CREDIT + w * NTILE + (n + 1))
                    one(k, w, 0, r, j, ACT.Square, j * P, "ssq", None)

            def one(k, w, p, r, j, func, cols, result, bias):
                n = p * PASS + r * NJ + j - 1
                act.wait_ge(sem("act_pass_1"), CREDIT + w * ACT_PASSES + (n - 1))
                x = SCOL[j]
                more = {"bias": bias} if bias is not None else {}
                nc.scalar.activation(b["junk", (n + k) % 2][:, 0:cols], b["S", k][:, r, x:x + cols], func,
                                     accum_out=b[result, k][:, r, j:j + 1], **more).then_inc(sem("act_pass_1"), 1)

            def signs(k, w, rnd):
                for r in range(2):
                    act.wait_ge(sem("t_ready_1"), CREDIT + (w * 3 + rnd) * 2 + (r + 1))
                    for j in range(1, NB):
                        one(k, w, rnd + 1, r, j, ACT.Sign, width(j), "cnt", b["nt", k][:, r, j:j + 1])

            def signs4(n, k, w):
                if 0 < n < NB:
                    if n == 1:
                        act.wait_ge(sem("t4_ready_1"), CREDIT + w * 2 + 1)
                    one(k, w, 4, 0, n, ACT.Sign, width(n), "cnt", b["nt", k][:, 0, n:n + 1])

            def exp1(n, k, w):
                r, j = divmod(n, NB)
                act.wait_ge(sem("max_ready_1"), CREDIT + w + 1)
                act.wait_ge(sem("p_ready_1"), CREDIT + w * NTILE + (n - NB + 1))
                x = SCOL[j]
                nc.scalar.activation(b["E"][:, x:x + width(j)], b["S", k][:, r, x:x + width(j)], ACT.Exp,
                                     bias=b["nmax", k][:, r, j:j + 1]).then_inc(sem("e_ready_1"), 1)

            def wave1(w, k, left):
                if left:
                    signs(1 - k, w + 1, 0)
                for n in range(NB // 2):
                    exp1(n, k, w)
                if left:
                    signs(1 - k, w + 1, 1)
                for n in range(NB // 2, NB):
                    exp1(n, k, w)
                if left:
                    signs(1 - k, w + 1, 2)
                for n in range(NTILE):
                    if NB <= n + NB - 1 < NTILE:
                        exp1(n + NB - 1, k, w)
                    for h in range(HALVES[n % NB]):
                        pt_copy(act, copy, l, b, n, w, h)
                    if n % 4 == 0 and n > 0:
                        ot_copy(n // 4 - 1, w)
                    if left:
                        signs4(n, 1 - k, w + 1)
                    if left == 2 and NB <= n < NTILE - 1:
                        square(2 * (n - NB), k, w + 2)
                        if n < NTILE - 2:
                            square(2 * (n - NB) + 1, k, w + 2)
                ot_copy(3, w)
                if left == 2:
                    for n in range(NTILE - 3, NTILE):
                        square(n, k, w + 2)
                store(k, w)

            act.wait_ge(sem(f"att_consts_{l}"), 1)
            if l == 0:
                credit(act, l, "p_ready", "pt_used1", "ot_copied")
                exp0(0, 0, 0)
                over_waves(act, wave0)
            else:
                credit(act, l, "pt_used0", "pt_used1", "ot_copied", "act_pass", "e_ready")
                for n in range(NTILE):
                    square(n, 0, 0)
                for rnd in range(3):
                    signs(0, 0, rnd)
                for n in range(NB):
                    signs4(n, 0, 0)
                for n in range(NTILE):
                    square(n, 1, 1)
                over_waves(act, wave1)

        def bracket(eng, e, b, tmp, k, rs, signed):
            target = TOP - 3.5
            up, down, dlo, dclo, dhi, dchi, move, step = (b[f"{tmp}{n}"][:, rs, 1:NB] for n in range(1, 9))
            c = {n: b[n, k][:, rs, 1:NB] for n in STATE}
            ts, tt = e.tensor_scalar, e.tensor_tensor
            cnt = b["cnt", k][:, signed, 1:NB]
            tt(cnt, cnt, b["cols"][:, signed, 1:NB], ALU.add)
            eng.drain()
            tt(cnt, cnt, b["half"][:, signed, 1:NB], ALU.mult)
            eng.drain()
            ts(up, c["cnt"], TOP + 0.25, None, ALU.is_gt)
            ts(down, c["cnt"], TOP - WINDOW + 0.75, None, ALU.is_lt)
            ts(step, c["cnt"], 1.0, -target, ALU.mult, ALU.add)
            ends = ((dlo, c["t"], c["lo"], up), (dclo, c["cnt"], c["clo"], up),
                    (dhi, c["t"], c["hi"], down), (dchi, c["cnt"], c["chi"], down))
            for d, new, old, _ in ends:
                tt(d, new, old, ALU.subtract)
            eng.drain()
            for d, _, _, flag in ends:
                tt(d, d, flag, ALU.mult)
            tt(step, step, c["kap"], ALU.mult)
            tt(c["blo"], c["blo"], up, ALU.add)
            tt(c["bhi"], c["bhi"], down, ALU.add)
            tt(move, up, down, ALU.add)
            eng.drain()
            for d, _, old, _ in ends:
                tt(old, old, d, ALU.add)
            eng.drain()
            both, span, counts, off, ahead = up, dlo, dclo, dhi, dchi
            tt(both, c["blo"], c["bhi"], ALU.mult)
            tt(span, c["hi"], c["lo"], ALU.subtract)
            tt(counts, c["clo"], c["chi"], ALU.subtract)
            tt(off, c["lo"], c["t"], ALU.subtract)
            ts(ahead, c["clo"], 1.0, -target, ALU.mult, ALU.add)
            eng.drain()
            ts(both, both, 1.0, 1.0, ALU.min, ALU.mult)
            tt(span, span, ahead, ALU.mult)
            ts(counts, counts, 1.0, 1.0, ALU.max, ALU.mult)
            tt(off, off, step, ALU.subtract)
            eng.drain()
            if eng is nc.gpsimd:
                tt(counts, counts, b["minus"][:, rs, 1:NB], ALU.pow)
            else:
                e.reciprocal(counts, counts)
            eng.drain()
            tt(span, span, counts, ALU.mult)
            eng.drain()
            tt(span, span, off, ALU.add)
            eng.drain()
            tt(span, span, both, ALU.mult)
            eng.drain()
            tt(step, step, span, ALU.add)
            eng.drain()
            tt(step, step, move, ALU.mult)
            eng.drain()
            tt(c["t"], c["t"], step, ALU.add)
            eng.drain()
            if eng is nc.gpsimd:
                ts(c["nt"], c["t"], -1.0, None, ALU.mult)
                eng.drain()

        def load_down(pool, b, c, k):
            cols = slice(k * D // 2, (k + 1) * D // 2)
            pool.dma_start(b["q"][:, :], down_q[bass.ts(c, P), cols]).then_inc(sem("dw_moved"), 16)
            for h in range(2):
                pool.dma_start(b["am"][64 * h:64 * h + 64, :],
                               down_am[bass.ds(c * 2 + h, 1), cols].to_broadcast([64, D // 2])
                               ).then_inc(sem("dw_moved"), 16)

        def dequantise_down(pool, b, c, k):
            pool.wait_ge(sem("dw_moved"), (c * 2 + k) * 64 + 48)
            nc.gpsimd.tensor_tensor(b["token"][:, :], b["token"][:, :], b["token"][:, :], ALU.mult)
            dequantise(pool, nc.gpsimd, *(b[n][:, :] for n in ("q", "am", "res", "sign", "mag", "acc")))
            pool.dma_start(wd_d[bass.ds(c, 1), :, k * D // 2:(k + 1) * D // 2].rearrange("a p n -> (a p) n"),
                           b["res"][:, :]).then_inc(sem("dw_moved"), 16)

        def down_chunks(pool, b, first, last):
            with pool.Fori(first, last) as c:
                for k in range(2):
                    load_down(pool, b, c, k)
                    dequantise_down(pool, b, c, k)

        def attend_gpsimd(pool, b, dw):
            g = nc.gpsimd
            PASS = 2 * (NB - 1)
            credit(pool, 1, "t_ready", "t4_ready")
            g.memset(b["half"][:, :, :], 0.5)
            g.memset(b["minus"][:, :, :], -1.0)
            for j in range(1, NB):
                g.memset(b["cols"][:, :, j:j + 1], float(width(j)))
            pool.drain()
            pool.wait_ge(sem("att_consts_1"), 1)
            pool.wait_ge(sem("tables_in"), 32)

            def wave(w, k):
                for r in range(2):
                    rs = slice(r, r + 1)
                    pool.wait_ge(sem("act_pass_1"), CREDIT + w * ACT_PASSES + (r + 1) * (NB - 1))
                    stand_alone(pool)
                    u1 = b["p1"][:, rs, 1:NB]
                    g.tensor_tensor(u1, b["ssq", k][:, rs, 1:NB], b["half"][:, rs, 1:NB], ALU.pow)
                    for n in ("blo", "bhi", "lo", "hi", "clo", "chi"):
                        g.memset(b[n, k][:, rs, 1:NB], 0.0)
                    pool.drain()
                    for name, tab in (("t", "quant"), ("kap", "kappa")):
                        g.tensor_tensor(b[name, k][:, rs, 1:NB], u1,
                                        b[tab][:, 1:NB].rearrange("p (a n) -> p a n", a=1), ALU.mult)
                    pool.drain()
                    g.tensor_scalar(b["nt", k][:, rs, 1:NB], b["t", k][:, rs, 1:NB], -1.0, None, ALU.mult)
                    pool.drain()
                    pool.sem_inc(sem("t_ready_1"), 1)
                for rnd in range(3):
                    for r in range(2):
                        pool.wait_ge(sem("act_pass_1"), CREDIT + w * ACT_PASSES + (rnd + 1) * PASS + (r + 1) * (NB - 1))
                        stand_alone(pool)
                        bracket(pool, g, b, "p", k, slice(r, r + 1), slice(r, r + 1))
                        if rnd < 2:
                            pool.sem_inc(sem("t_ready_1"), 1)
                        else:
                            pool.sem_inc(sem("t4_ready_1"), 1)
            with pool.Fori(0, MC - DOWN_EARLY) as t:
                for k in range(2):
                    load_down(pool, dw, t + DOWN_EARLY, k)
                    wave(t * 2 + k, k)
                    dequantise_down(pool, dw, t + DOWN_EARLY, k)
            with pool.Fori(MC - DOWN_EARLY, WAVES // 2) as t:
                for k in range(2):
                    wave(t * 2 + k, k)
            pool.wait_ge(sem("dw_moved"), 64 * 2 * MC)

        def attend_vector(v, l, b):
            dve = nc.vector

            def out_rows(m, k, w):
                r, j0 = (4 * m) // NB, (4 * m) % NB
                v.wait_ge(sem(f"rows_done_{l}"), CREDIT + w * 4 + (m + 1))
                if l == 0:
                    v.wait_ge(sem("p_ready_0"), CREDIT + w * NTILE + (4 * m + 4))
                dve.reciprocal(b["rsum", k][:, r, j0:j0 + 4], b["sum", k][:, r, j0:j0 + 4])
                v.drain()
                if m == 0:
                    v.wait_ge(sem(f"o_out{k}_{l}"), ONE_DMA + (w - k) * 8)
                dve.tensor_tensor(b["O", k][:, j0:j0 + 4, r * HD:(r + 1) * HD], OQ_PS,
                                  b["rsum", k][:, r, j0:j0 + 4].rearrange("p (a o) -> p a o", o=1).to_broadcast([P, 4, HD]),
                                  ALU.mult)
                v.drain().then_inc(sem(f"oq_read_{l}"), 1)
                v.sem_inc(sem(f"o_ready_{l}"), 1)

            for k in range(2):
                dve.memset(b["V", k][:, :, HD:32], 0.0)
            dve.memset(b["zeroV"][:, :], 0.0)
            if l == 0:
                credit(v, l, "max_ready", "oq_read", "o_ready", "pt_used0")
                v.drain().then_inc(sem("att_consts_0"), 1)

                def maxes(n, k, w):
                    r, j = divmod(n, NB)
                    v.wait_ge(sem("s_done_0"), CREDIT + w * NTILE + (n + 1))
                    dve.tensor_reduce(b["nmax", k][:, r, j:j + 1], s_ps(n)[:, 0:width(j)], AX.X, ALU.max,
                                      negate=True).then_inc(sem("max_ready_0"), 1)

                def wave0(w, k, left):
                    for n in range(NTILE):
                        if n + 2 < NTILE:
                            maxes(n + 2, k, w)
                        elif left:
                            maxes(n + 2 - NTILE, 1 - k, w + 1)
                        pt_copy(v, dve.tensor_copy, l, b, n, w, 0)
                        if n % 4 == 1 and n > 1:
                            out_rows(n // 4 - 1, k, w)
                    out_rows(3, k, w)
                for n in range(2):
                    maxes(n, 0, 0)
                over_waves(v, wave0)
                return

            credit(v, l, "s_stored", "max_ready", "p_ready", "oq_read", "o_ready")
            for e in range(8):
                dve.memset(b["iota8"][:, e:e + 1], float(e))
            dve.memset(b["theta"][:, :, :], NEG / 10)
            dve.memset(b["open"][:, :], 0.0)
            v.drain().then_inc(sem("att_consts_1"), 1)

            def store_scores(n, k, w):
                r, j = divmod(n, NB)
                x = SCOL[j]
                v.wait_ge(sem("s_done_1"), CREDIT + w * NTILE + (n + 1))
                dve.tensor_scalar(b["S", k][:, r, x:x + width(j)], s_ps(n)[:, 0:width(j)], 1.0, None, ALU.mult,
                                  ALU.max, accum_out=b["max", k][:, r, j:j + 1]).then_inc(sem("s_stored_1"), 1)

            def end_store(k):
                v.drain()
                dve.tensor_scalar(b["nmax", k][:, :, :], b["max", k][:, :, :], -1.0, None, ALU.mult)
                v.drain().then_inc(sem("max_ready_1"), 1)

            def window(k, w):
                tiles = [(r, j) for r in range(2) for j in range(1, NB)]
                for n in range(len(tiles) + 2):
                    v.drain()
                    for stage in range(3):
                        q = n - stage
                        if not 0 <= q < len(tiles):
                            continue
                        r, j = tiles[q]
                        y = b["Y", q % 3][:, 0:width(j)]
                        sc = b["S", k][:, r, SCOL[j]:SCOL[j] + width(j)]
                        if stage == 0:
                            dve.tensor_scalar(y, sc, b["t", k][:, r, j:j + 1], None, ALU.is_ge, ALU.add,
                                              accum_out=b["cnt", k][:, r, j:j + 1])
                        elif stage == 1:
                            dve.scalar_tensor_tensor(y, y, NEG, sc, ALU.mult, ALU.add)
                        else:
                            dve.max(b["top8"][:, r, j, :], y)
                v.drain()

            def choose(k):
                c = {n: b[n, k][:, :, 1:NB] for n in STATE}
                u1, u2, u3, u4 = (b[f"v{n}"][:, :, 1:NB] for n in range(1, 5))
                pick, top, after = b["pick"], b["top8"], b["after"]

                def each(ap):
                    return ap.rearrange("p (a n) -> p a n", n=1).to_broadcast([P, NB - 1, 8])
                dve.tensor_scalar(u1, c["cnt"], -1.0, TOP - 1.0, ALU.mult, ALU.add)
                dve.tensor_scalar(u2, c["cnt"], float(TOP), None, ALU.is_equal)
                dve.tensor_scalar(u3, c["cnt"], TOP - WINDOW + 0.5, None, ALU.is_ge)
                dve.tensor_scalar(u4, c["cnt"], TOP + 0.5, None, ALU.is_lt)
                v.drain()
                for r in range(2):
                    dve.tensor_tensor(pick[:, r, 1:NB, :],
                                      b["iota8"][:, :].rearrange("p (a n) -> p a n", a=1).to_broadcast([P, NB - 1, 8]),
                                      each(b["v1"][:, r, 1:NB]), ALU.is_equal)
                dve.tensor_tensor(u2, u2, c["t"], ALU.mult)
                dve.tensor_tensor(u3, u3, u4, ALU.mult)
                v.drain()
                for r in range(2):
                    dve.tensor_tensor(pick[:, r, 1:NB, :], pick[:, r, 1:NB, :], top[:, r, 1:NB, :], ALU.mult)
                v.drain()
                for r in range(2):
                    dve.tensor_reduce(b["theta"][:, r, 1:NB], pick[:, r, 1:NB, :], AX.X, ALU.add)
                v.drain()
                dve.tensor_tensor(b["theta"][:, :, 1:NB], b["theta"][:, :, 1:NB], u2, ALU.add)
                v.drain()
                for r in range(2):
                    dve.tensor_tensor(after[:, r, 1:NB, :], top[:, r, 1:NB, :], each(b["theta"][:, r, 1:NB]), ALU.is_ge)
                v.drain()
                for r in range(2):
                    dve.tensor_reduce(b["v4"][:, r, 1:NB], after[:, r, 1:NB, :], AX.X, ALU.add)
                v.drain()
                dve.tensor_tensor(u4, u4, c["cnt"], ALU.add)
                v.drain()
                dve.tensor_scalar(u4, u4, float(TOP), None, ALU.is_equal)
                v.drain()
                dve.tensor_tensor(b["settled"][:, :, 1:NB], u3, u4, ALU.mult)
                v.drain()
                dve.tensor_reduce(b["open"][:, 0:1], b["settled"][:, :, 1:NB], AX.XY, ALU.min)
                v.drain()
                dve.tensor_scalar(b["open"][:, 0:1], b["open"][:, 0:1], -1.0, 1.0, ALU.mult, ALU.add)
                v.drain()
                dve.transpose(b["openT"][:, :], b["open"][:, :])
                v.drain()
                dve.tensor_reduce(b["row"][:, :], b["openT"][:, :], AX.X, ALU.max)
                v.drain()
                for q in range(4):
                    dve.tensor_copy(b["openT"][0:1, q:q + 1], b["row"][32 * q:32 * q + 1, :])
                v.drain()
                dve.tensor_reduce(b["any"][:, :], b["openT"][0:1, 0:4], AX.X, ALU.max)
                v.drain()

            def select(k, w):
                left_open = v.value_load(b["any"][:, :], min_val=0, max_val=1)
                with v.If(left_open > 0):
                    v.wait_ge(sem("e_ready_1"), CREDIT + w * NTILE + NB)
                    for r in range(2):
                        for j in range(1, NB):
                            y, sc = b["Y", 0][:, 0:width(j)], b["S", k][:, r, SCOL[j]:SCOL[j] + width(j)]
                            dve.tensor_copy(y, sc)
                            v.drain()
                            with v.Fori(0, TOP // 8):
                                dve.max(b["top8"][:, r, j, :], y)
                                v.drain()
                                dve.match_replace(y, b["top8"][:, r, j, :], y, TAKEN)
                                v.drain()
                            dve.tensor_scalar(y, y, TAKEN, NEG, ALU.not_equal, ALU.mult)
                            v.drain()
                            dve.tensor_tensor(sc, sc, y, ALU.add)
                            v.drain()
                    dve.memset(b["theta"][:, :, :], NEG / 10)
                    v.drain()

            def count4(k, w):
                v.wait_ge(sem("t4_ready_1"), CREDIT + w * 2 + 2)
                for j in range(1, NB):
                    if j % 3 == 1 and j > 1:
                        v.drain()
                    dve.tensor_scalar(b["Y", j % 3][:, 0:width(j)], b["S", k][:, 1, SCOL[j]:SCOL[j] + width(j)],
                                      b["t", k][:, 1, j:j + 1], None, ALU.is_ge, ALU.add,
                                      accum_out=b["cnt", k][:, 1, j:j + 1])
                v.drain()
                v.wait_ge(sem("act_pass_1"), CREDIT + (w + 1) * ACT_PASSES)
                bracket(v, dve, b, "v", k, slice(0, 2), slice(0, 1))

            def products(k, w, left):
                for n in range(NTILE):
                    r, j = divmod(n, NB)
                    x = SCOL[j]
                    v.wait_ge(sem("e_ready_1"), CREDIT + w * NTILE + (n + 1))
                    before = PT_AT[n - 1] if n >= 2 else PT_AT[n + NTILE - 1] - PT_WAVE
                    v.wait_ge(sem("turned_1"), CREDIT + w * PT_WAVE + before)
                    dve.scalar_tensor_tensor(b["P", n % 2][:, 0:width(j)], b["S", k][:, r, x:x + width(j)],
                                             b["theta"][:, r, j:j + 1], b["E"][:, x:x + width(j)],
                                             ALU.is_ge, ALU.mult,
                                             accum_out=b["sum", k][:, r, j:j + 1]).then_inc(sem("p_ready_1"), 1)
                    if left == 2 and n > 0:
                        v.wait_ge(sem("p_ready_1"), CREDIT + w * NTILE + n)
                        store_scores(n - 1, k, w + 2)
                    if n % 4 == 2 and n > 2:
                        out_rows(n // 4 - 1, k, w)
                if left == 2:
                    v.wait_ge(sem("p_ready_1"), CREDIT + w * NTILE + NTILE)
                    store_scores(NTILE - 1, k, w + 2)

            def wave1(w, k, left):
                count4(k, w)
                window(k, w)
                choose(k)
                select(k, w)
                products(k, w, left)
                out_rows(3, k, w)
                if left == 2:
                    end_store(k)

            for w in range(2):
                for n in range(NTILE):
                    store_scores(n, w, w)
                end_store(w)
            over_waves(v, wave1)

        def output_buffers(c, l):
            b = {}
            for k in range(2):
                b["o", k] = sb(c, f"o{l}{k}", [P, D])
                b["oT", k] = sb(c, f"oT{l}{k}", [P, KC, P])
                b["res", k] = sb(c, f"res{l}{k}", [P, D])
            b["wo"] = sb(c, f"wo{l}", [P, KC, D])
            return b

        def ot_bank(k):
            return banks[:, k, :].rearrange("p (c n) -> p c n", c=KC)

        def output_sync(eng, l, b, wo):
            if l == 1:
                credit_dma(eng, "out0", "out1")
            eng.dma_start(b["wo"][:, :, :], wo.rearrange("(c p) n -> p c n", p=P)).then_inc(sem(f"wo_in_{l}"), 16)

            def load(pos, seq, k):
                src = o_d[l][seq * (WAVES // 2):(seq + 1) * (WAVES // 2), bass.ts(pos, P), :]
                eng.dma_start(b["o", k][:, :].rearrange("p (w d) -> p w d", d=2 * HD),
                              src.rearrange("w p d -> p w d")).then_inc(sem(f"o_in{k}_{l}"), 16)

            def store(i, k):
                if l == 1:
                    eng.wait_ge(sem("y_added_1"), CREDIT + i + 1)
                    stand_alone(eng)
                    eng.dma_start(out[bass.ts(i, P), :], b["res", k][:, :]).then_inc(sem(f"out{k}"), 16)

            for k in range(2):
                load(k, 0, k)
            for seq in range(2):
                with eng.Fori(0, NB // 2 - 1) as t:
                    for k in range(2):
                        i = t * 2 + (k + seq * NB)
                        eng.wait_ge(sem(f"o_turned_{l}"), CREDIT + i + 1)
                        stand_alone(eng)
                        load(t * 2 + k + 2, seq, k)
                        store(i, k)
                for k in range(2):
                    i = (seq + 1) * NB - 2 + k
                    if seq == 0:
                        eng.wait_ge(sem(f"o_turned_{l}"), CREDIT + i + 1)
                        load(k, 1, k)
                    store(i, k)
            if l == 1:
                for k in range(2):
                    eng.wait_ge(sem(f"out{k}"), ONE_DMA + 16 * NT // 2)

        def output_tensor(pe, l, b):
            def turn(i, k):
                pe.wait_ge(sem(f"o_in{k}_{l}"), (i - k) * 8 + 16)
                pe.wait_ge(sem(f"oT_ready_{l}"), CREDIT + i - 1)
                for c in range(KC):
                    mm = nc.tensor.transpose(ot_bank(k)[:, c, :], b["o", k][:, c * P:(c + 1) * P], identf[:, :])
                mm.then_inc(sem(f"o_turned_{l}"), 1)

            credit(pe, l, "o_turned", "y_done")
            pe.wait_ge(sem(f"wo_in_{l}"), 16)
            turn(0, 0)

            def body(i, pos, seq, k, last):
                if not last:
                    turn(i + 1, 1 - k)
                pe.wait_ge(sem(f"oT_ready_{l}"), CREDIT + i + 1)
                pe.wait_ge(sem(f"y_added_{l}"), CREDIT + i - 1)
                for c in range(KC):
                    mm = nc.tensor.matmul(banks[:, 2 + k, :], b["oT", k][:, c, :], b["wo"][:, c, :],
                                          start=(c == 0), stop=(c == KC - 1))
                mm.then_inc(sem(f"y_done_{l}"), 1)
            over_tiles(pe, body)

        def output_scalar(act, l, b):
            credit(act, l, "oT_ready")

            def body(i, pos, seq, k, last):
                act.wait_ge(sem(f"o_turned_{l}"), CREDIT + i + 1)
                act.wait_ge(sem(f"y_done_{l}"), CREDIT + i - 1)
                nc.scalar.activation(b["oT", k][:, :, :], ot_bank(k), ACT.Copy).then_inc(sem(f"oT_ready_{l}"), 1)
            over_tiles(act, body)

        def output_vector(v, l, b):
            credit(v, l, "y_added")

            def body(i, pos, seq, k, last):
                v.wait_ge(sem(f"y_done_{l}"), CREDIT + i + 1)
                if l == 1:
                    v.wait_ge(sem(f"out{k}"), ONE_DMA + (i - k) * 8)
                dst = b["res", k][:, :] if l else token_tile(i)
                nc.vector.tensor_tensor(dst, banks[:, 2 + k, :], token_tile(i), ALU.add)
                v.drain().then_inc(sem(f"y_added_{l}"), 1)
            over_tiles(v, body)

        def ffn_buffers(c):
            b = {}
            b["w"] = sb(c, "w_gu", [P, 2, KC, M])
            b["wd"] = sb(c, "w_down", [P, MC, D])
            b["h"] = sb(c, "h", [P, MC, TW])
            for k in range(2):
                b["x", k] = sb(c, f"ffn_x{k}", [P, KC, TW])
                b["sil", k] = sb(c, f"sil{k}", [P, TW])
            return b

        def ffn_sync(eng, b):
            def load_x(k, tb):
                eng.dma_start(b["x", k][:, :, :], xT_d[:, :, tb * TW:(tb + 1) * TW]).then_inc(sem(f"ffx_in{k}"), 16)
            load_x(0, 0)
            for n in range(MC // 2):
                cols = slice(n * 2 * P, (n + 1) * 2 * P)
                for u in range(2):
                    eng.dma_start(b["w"][:, u, :, cols],
                                  w_d[u].rearrange("c p n -> p c n")[:, :, cols]).then_inc(sem(f"w_in{n}"), 16)
            load_x(1, 1)
            eng.dma_start(b["wd"][:, :, :], wd_d.rearrange("c p n -> p c n")).then_inc(sem("wd_in"), 16)
            for k in range(2):
                eng.wait_ge(sem("gu_done_f"), CREDIT + (k + 1) * MC)
                stand_alone(eng)
                load_x(k, k + 2)

        def ffn_tensor(pe, b):
            credit(pe, "f", "gu_done", "down_done")
            with pe.Fori(0, TB // 2) as t:
                for k in range(2):
                    tb = t * 2 + k
                    pe.wait_ge(sem(f"ffx_in{k}"), t * 16 + 16)
                    for m in range(MC):
                        pe.wait_ge(sem(f"w_in{m // 2}"), 16 * 2)
                        pe.wait_ge(sem("h_ready_f"), CREDIT + tb * MC + (m - 1))
                        for u in range(2):
                            for c in range(KC):
                                mm = nc.tensor.matmul(banks[:, 2 * u + m % 2, :], b["w"][:, u, c, m * P:(m + 1) * P],
                                                      b["x", k][:, c, :], start=(c == 0), stop=(c == KC - 1))
                        mm.then_inc(sem("gu_done_f"), 1)
                    pe.wait_ge(sem("wd_in"), 16)
                    pe.wait_ge(sem("h_ready_f"), CREDIT + (tb + 1) * MC)
                    for a in range(TW // P):
                        pe.wait_ge(sem("down_added_f"), CREDIT + tb * (TW // P) + (a - 3))
                        for m in range(MC):
                            mm = nc.tensor.matmul(banks[:, 4 + a, :], b["h"][:, m, a * P:(a + 1) * P], b["wd"][:, m, :],
                                                  start=(m == 0), stop=(m == MC - 1))
                        mm.then_inc(sem("down_done_f"), 1)

        def ffn_scalar(act, b):
            credit(act, "f", "sil_ready")
            with act.Fori(0, TB) as tb:
                for m in range(MC):
                    act.wait_ge(sem("gu_done_f"), CREDIT + tb * MC + (m + 1))
                    act.wait_ge(sem("h_ready_f"), CREDIT + tb * MC + (m - 1))
                    nc.scalar.activation(b["sil", m % 2][:, :], banks[:, m % 2, :], ACT.Silu).then_inc(sem("sil_ready_f"), 1)

        def ffn_vector(v, b):
            dve = nc.vector
            credit(v, "f", "h_ready", "down_added")
            with v.Fori(0, TB) as tb:
                for m in range(MC):
                    v.wait_ge(sem("sil_ready_f"), CREDIT + tb * MC + (m + 1))
                    v.wait_ge(sem("down_done_f"), CREDIT + tb * (TW // P))
                    dve.tensor_tensor(b["h"][:, m, :], banks[:, 2 + m % 2, :], b["sil", m % 2][:, :],
                                      ALU.mult).then_inc(sem("h_ready_f"), 1)
                for a in range(TW // P):
                    i = tb * (TW // P) + a
                    v.wait_ge(sem("down_done_f"), CREDIT + i + 1)
                    dve.tensor_tensor(token_tile(i), banks[:, 4 + a, :], token_tile(i), ALU.add).then_inc(
                        sem("down_added_f"), 1)

        layers = [(wqkv0, wo0), (wqkv1, wo1)]
        dw = {"q": sb(ctx, "dw_q", [P, D // 2], I32), "token": sb(ctx, "dw_token", [P, 1])}
        for n in ("am", "res", "sign", "mag", "acc"):
            dw[n] = sb(ctx, f"dw_{n}", [P, D // 2])
        dq_ctx = ExitStack()
        dq = {}
        for k in range(2):
            dq["q", k] = sb(dq_ctx, f"dq_q{k}", [P, DQ], I32)
            dq["am", k] = sb(dq_ctx, f"dq_am{k}", [P, DQ])
            dq["res", k] = sb(dq_ctx, f"dq_res{k}", [P, DQ])
        for n in ("sign", "mag", "acc"):
            dq[n] = sb(dq_ctx, f"dq_{n}", [P, DQ])
        dq["token"] = sb(dq_ctx, "dq_token", [P, 1])
        bufs = {}
        for l in (0, 1):
            for name, make in (("project", project_buffers), ("attend", attend_buffers)):
                with ExitStack() as c:
                    bufs[name, l] = make(c, l)
            if l == 1:
                with ExitStack() as c:
                    bufs["ffn"] = ffn_buffers(c)
            with ExitStack() as c:
                bufs["output", l] = output_buffers(c, l)
            if l == 0:
                dq_ctx.close()

        block = ctx.enter_context(nc.Block())

        @block.sync
        def _(sp):
            sp.sem_inc(sem("started"), 1)
            for l, (wqkv, wo) in enumerate(layers):
                project_sync(sp, l, bufs["project", l], wqkv)
                barrier(sp, 4 * l + 1)
                attend_sync(sp, l, bufs["attend", l])
                barrier(sp, 4 * l + 2)
                if l == 1:
                    ffn_sync(sp, bufs["ffn"])
                barrier(sp, 4 * l + 3)
                output_sync(sp, l, bufs["output", l], wo)
                barrier(sp, 4 * l + 4)

        @block.tensor
        def _(pe):
            for l in (0, 1):
                project_tensor(pe, l, bufs["project", l])
                barrier(pe, 4 * l + 1)
                attend_tensor(pe, l, bufs["attend", l])
                barrier(pe, 4 * l + 2)
                if l == 1:
                    ffn_tensor(pe, bufs["ffn"])
                barrier(pe, 4 * l + 3)
                output_tensor(pe, l, bufs["output", l])
                barrier(pe, 4 * l + 4)

        @block.scalar
        def _(act):
            for l in (0, 1):
                project_scalar(act, l, bufs["project", l])
                barrier(act, 4 * l + 1)
                attend_scalar(act, l, bufs["attend", l])
                barrier(act, 4 * l + 2)
                if l == 1:
                    ffn_scalar(act, bufs["ffn"])
                barrier(act, 4 * l + 3)
                output_scalar(act, l, bufs["output", l])
                barrier(act, 4 * l + 4)

        @block.vector
        def _(v):
            for l in (0, 1):
                project_vector(v, l, bufs["project", l])
                barrier(v, 4 * l + 1)
                attend_vector(v, l, bufs["attend", l])
                barrier(v, 4 * l + 2)
                if l == 1:
                    ffn_vector(v, bufs["ffn"])
                barrier(v, 4 * l + 3)
                output_vector(v, l, bufs["output", l])
                barrier(v, 4 * l + 4)

        @block.gpsimd
        def _(pool):
            dequantise_gate_up(pool, dq)
            nc.gpsimd.memset(dw["token"][:, :], 0.0)
            pool.drain()
            down_chunks(pool, dw, 0, 2)
            barrier(pool, POOL_JOINS)
            down_chunks(pool, dw, 2, DOWN_EARLY)
            barrier(pool, POOL_JOINS + 1)
            attend_gpsimd(pool, bufs["attend", 1], dw)
            for n in range(6, 9):
                barrier(pool, n)


NF4 = [-1.0, -0.6961928009986877, -0.5250730514526367, -0.39491748809814453, -0.28444138169288635,
       -0.18477343022823334, -0.09105003625154495, 0.0, 0.07958029955625534, 0.16093020141124725,
       0.24611230194568634, 0.33791524171829224, 0.44070982933044434, 0.5626170039176941,
       0.7229568362236023, 1.0]


def shape_constants():
    import numpy as np
    from math import erf, exp, pi
    inv = (np.float32(1.0) / np.float32(10000.0) ** (np.arange(0, HD, 2, dtype=np.float32) / np.float32(HD))).astype(np.float32)
    angle = np.arange(SEQ, dtype=np.float32)[:, None] * inv[None, :]
    cos, sin = (np.float32(0.5) * f(angle).astype(np.float32) for f in (np.cos, np.sin))

    def normal_quantile(q):
        lo, hi = -10.0, 10.0
        for _ in range(60):
            mid = (lo + hi) / 2
            if 0.5 + 0.5 * erf(mid / 2 ** 0.5) < q:
                lo = mid
            else:
                hi = mid
        return lo

    quantile, kappa = np.zeros((P, NB), np.float32), np.zeros((P, NB), np.float32)
    for j in range(1, NB):
        for p in range(P):
            length = j * P + p + 1
            z = -normal_quantile((TOP - 4.0) / length)
            quantile[p, j] = z / (j * P) ** 0.5
            kappa[p, j] = (2 * pi) ** 0.5 * exp(z * z / 2) / length / (j * P) ** 0.5
    code = np.array(NF4)
    above, below = code[8:], -code[7::-1]
    at = np.vander(np.arange(8) - 3.5, 8)
    poly = [[float(np.float32(c)) for c in np.linalg.solve(at, y)] for y in ((above + below) / 2, (above - below) / 2)]
    return {
        "rope_cos": cos, "rope_sin": sin, "ident": np.eye(P, dtype=np.float32),
        "causal": np.where(np.arange(P)[:, None] < np.arange(P)[None, :], np.float32(NEG), np.float32(0)),
        "quantile": quantile, "kappa": kappa,
    }, poly


def lay_out(a):
    import numpy as np
    c = np.ascontiguousarray
    return {
        "x": c(a["L0_attn_x"].reshape(T, D)),
        "wqkv0": c(a["L0_attn_w_qkv"]), "wo0": c(a["L0_attn_w_o"]),
        "wup": c(a["L0_ffn_W_up"].T),
        "gate_lora": c(np.concatenate([a["L0_ffn_gate_w"], a["L0_ffn_lora_A"].reshape(NE * NR, D)]).T),
        "expert_bias": c(a["L0_ffn_expert_bias"].reshape(1, NE)),
        "lora_b": c(a["L0_ffn_lora_B"].transpose(0, 2, 1).reshape(NE * NR, D)),
        "wqkv1": c(np.concatenate([a["L1_attn_Wq"], a["L1_attn_Wk"], a["L1_attn_Wv"]]).T),
        "wo1": c(a["L1_attn_Wo"].T),
        "gate_q": c(a["L1_ffn_gate_q"].T), "gate_am": c(a["L1_ffn_gate_absmax"].reshape(M, D // 64).T),
        "up_q": c(a["L1_ffn_up_q"].T), "up_am": c(a["L1_ffn_up_absmax"].reshape(M, D // 64).T),
        "down_q": c(a["L1_ffn_down_q"].T), "down_am": c(a["L1_ffn_down_absmax"].reshape(D, M // 64).T),
    }


def kernel(**inputs):
    import numpy as np
    import concourse.bacc as bacc
    from concourse.bass_utils import run_bass_kernel_spmd

    constants, poly = shape_constants()
    arrays = {**lay_out({k: np.asarray(v) for k, v in inputs.items()}), **constants}
    nc = bacc.Bacc("TRN2", target_bir_lowering=False, num_devices=1)
    args = {n: nc.dram_tensor(f"in_{n}", a.shape, mybir.dt.from_np(a.dtype), kind="ExternalInput").ap()
            for n, a in arrays.items()}
    out = nc.dram_tensor("out_y", (T, D), F32, kind="ExternalOutput").ap()
    kernel_program(nc, poly, out=out, **args)
    r = run_bass_kernel_spmd(nc, [{f"in_{n}": a for n, a in arrays.items()}], core_ids=[0])
    return r.results[0]["out_y"].reshape(2, SEQ, D)
```
